# Optimizing a Trainium2 kernel written in Bass

```python
import numpy as np
import jax
import jax.numpy as jnp

def _softmax(x, axis=-1):
    return jax.nn.softmax(x, axis=axis)

def _gelu(x):
    return jax.nn.gelu(x, approximate=True)

def _silu(x):
    return jax.nn.silu(x)

def _sigmoid(x):
    return jax.nn.sigmoid(x)

def _layernorm(x, axis=-1, eps=1e-05):
    m = jnp.mean(x, axis=axis, keepdims=True)
    v = jnp.var(x, axis=axis, keepdims=True)
    return (x - m) / jnp.sqrt(v + eps)

def _scatter_add(tgt, idx, src, axis=0):
    return tgt.at[idx].add(src)

def _segment_sum(src, seg, n):
    return jax.ops.segment_sum(src, seg, n)
kernel_name = 'mk_adj_preln_d2_adj_r2_700eb2'

def setup_inputs(seed: int=0):
    np.random.seed(seed)
    _w = jnp.asarray

    def _rec_inputs():
        import jax
        import jax.numpy as jnp
        _gk = jax.random.key(seed)
        x = -0.001003 + 1 * jax.random.normal(jax.random.fold_in(_gk, 1), (6144, 128), jnp.float32)
        _w = (1.0 + jnp.arange(6144, dtype=jnp.float32)) ** (-0.5)
        _w = _w / _w.mean()
        _pij = jnp.clip(0.000325521 * _w[:, None] * _w[None, :], 0.0, 1.0)
        _a = jax.random.uniform(jax.random.fold_in(_gk, 2), (6144, 6144)) < _pij
        _a = jnp.logical_or(_a, jnp.eye(6144, dtype=bool))
        _af = _a.astype(jnp.float32)
        _af = _af * jax.random.uniform(jax.random.fold_in(_gk, 3), (6144, 6144), jnp.float32, 0.05, 1)
        adj = _af
        return (x, adj)
    x, adj = _rec_inputs()

    def _L0_gnn_setup():
        import jax, jax.numpy as jnp
        import numpy as np
        TAU = 1.0
        EPS = 1e-10
        LN_EPS = 1e-05

        def _layernorm(x, g, b):
            m = jnp.mean(x, axis=-1, keepdims=True)
            v = jnp.mean((x - m) ** 2, axis=-1, keepdims=True)
            return (x - m) * jax.lax.rsqrt(v + LN_EPS) * g + b
        key = jax.random.key(seed)
        N, D = (6144, 128)
        ks = jax.random.split(key, 12)
        s = 1.0 / np.sqrt(D)
        inp = {'x': jax.random.normal(ks[0], (N, D), jnp.float32), 'adj': jax.random.uniform(ks[1], (N, N), jnp.float32), 'u': jax.random.uniform(ks[2], (N, 2), jnp.float32), 'W1': jax.random.normal(ks[3], (D, D), jnp.float32) * s, 'b1': jnp.zeros((D,), jnp.float32), 'W2': jax.random.normal(ks[4], (D, D), jnp.float32) * s, 'b2': jnp.zeros((D,), jnp.float32), 'Wg': jax.random.normal(ks[5], (2 * D, D), jnp.float32) * s, 'bg': jnp.zeros((D,), jnp.float32), 'Wn': jax.random.normal(ks[6], (D, 2), jnp.float32) * s, 'bn': jnp.zeros((2,), jnp.float32), 'g_in': jnp.ones((D,), jnp.float32), 'b_in': jnp.zeros((D,), jnp.float32), 'g_out': jnp.ones((D,), jnp.float32), 'b_out': jnp.zeros((D,), jnp.float32)}
        return inp
    _L0_gnn_all = _L0_gnn_setup()
    _L0_gnn_in = {k: v for k, v in _L0_gnn_all.items() if k in ('u', 'W1', 'b1', 'W2', 'b2', 'Wg', 'bg', 'Wn', 'bn', 'g_in', 'b_in', 'g_out', 'b_out')}
    del _L0_gnn_all

    def _L1_gnn_setup():
        import jax, jax.numpy as jnp
        import numpy as np
        N, DIN, DOUT = (4096, 128, 128)
        NEG = -9000000000000000.0
        ALPHA = 0.2
        key = jax.random.key(seed)
        kx, ka, kw, ks, kr = jax.random.split(key, 5)
        X = jax.random.normal(kx, (N, DIN), dtype=jnp.float32)
        A = (jax.random.uniform(ka, (N, N)) < 0.01).astype(jnp.float32)
        A = A.at[jnp.arange(N), jnp.arange(N)].set(1.0)
        lim_w = float(np.sqrt(6.0 / (DIN + DOUT)))
        W = jax.random.uniform(kw, (DOUT, DIN), jnp.float32, -lim_w, lim_w)
        b = jnp.zeros((DOUT,), jnp.float32)
        lim_a = float(np.sqrt(6.0 / (DOUT + 1)))
        a_s = jax.random.uniform(ks, (DOUT, 1), jnp.float32, -lim_a, lim_a)
        a_r = jax.random.uniform(kr, (DOUT, 1), jnp.float32, -lim_a, lim_a)
        return {'X': X, 'A': A, 'W': W, 'b': b, 'a_s': a_s, 'a_r': a_r}
    _L1_gnn_all = _L1_gnn_setup()
    _L1_gnn_in = {k: v for k, v in _L1_gnn_all.items() if k in ('W', 'b', 'a_s', 'a_r')}
    del _L1_gnn_all
    return {'x': x, 'adj': adj, 'L0_gnn_u': _L0_gnn_in['u'], 'L0_gnn_W1': _L0_gnn_in['W1'], 'L0_gnn_b1': _L0_gnn_in['b1'], 'L0_gnn_W2': _L0_gnn_in['W2'], 'L0_gnn_b2': _L0_gnn_in['b2'], 'L0_gnn_Wg': _L0_gnn_in['Wg'], 'L0_gnn_bg': _L0_gnn_in['bg'], 'L0_gnn_Wn': _L0_gnn_in['Wn'], 'L0_gnn_bn': _L0_gnn_in['bn'], 'L0_gnn_g_in': _L0_gnn_in['g_in'], 'L0_gnn_b_in': _L0_gnn_in['b_in'], 'L0_gnn_g_out': _L0_gnn_in['g_out'], 'L0_gnn_b_out': _L0_gnn_in['b_out'], 'L1_gnn_W': _L1_gnn_in['W'], 'L1_gnn_b': _L1_gnn_in['b'], 'L1_gnn_a_s': _L1_gnn_in['a_s'], 'L1_gnn_a_r': _L1_gnn_in['a_r']}

def reference(x, adj, L0_gnn_u, L0_gnn_W1, L0_gnn_b1, L0_gnn_W2, L0_gnn_b2, L0_gnn_Wg, L0_gnn_bg, L0_gnn_Wn, L0_gnn_bn, L0_gnn_g_in, L0_gnn_b_in, L0_gnn_g_out, L0_gnn_b_out, L1_gnn_W, L1_gnn_b, L1_gnn_a_s, L1_gnn_a_r):
    import jax
    import jax.numpy as jnp

    def _L0_gnn_ref(x, adj, u, W1, b1, W2, b2, Wg, bg, Wn, bn, g_in, b_in, g_out, b_out):
        import jax, jax.numpy as jnp
        import numpy as np
        TAU = 1.0
        EPS = 1e-10
        LN_EPS = 1e-05

        def _layernorm(x, g, b):
            m = jnp.mean(x, axis=-1, keepdims=True)
            v = jnp.mean((x - m) ** 2, axis=-1, keepdims=True)
            return (x - m) * jax.lax.rsqrt(v + LN_EPS) * g + b
        residual = x
        x_norm = _layernorm(x, g_in, b_in)
        logits = x_norm @ Wn + bn
        gumbel = -jnp.log(-jnp.log(jnp.clip(u, EPS, 1.0)) + EPS)
        y_soft = jax.nn.softmax((logits + gumbel) / TAU, axis=-1)
        hard = jax.nn.one_hot(jnp.argmax(y_soft, axis=-1), 2, dtype=y_soft.dtype)
        y = hard + y_soft - jax.lax.stop_gradient(y_soft)
        gate = y[:, 1]
        sel_adj = adj * gate[:, None] * gate[None, :]
        view1 = x_norm
        view2 = sel_adj @ x_norm
        fusion_gate = jax.nn.sigmoid(jnp.concatenate([view1, view2], axis=-1) @ Wg + bg)
        fused = fusion_gate * (view1 @ W1 + b1) + (1.0 - fusion_gate) * (view2 @ W2 + b2)
        return _layernorm(fused + residual, g_out, b_out)

    def _L1_gnn_ref(X, A, W, b, a_s, a_r):
        import jax, jax.numpy as jnp
        import numpy as np
        N, DIN, DOUT = (4096, 128, 128)
        NEG = -9000000000000000.0
        ALPHA = 0.2
        H = X @ W.T + b
        s = H @ a_s
        r = H @ a_r
        e = jax.nn.leaky_relu(A * s + A * r.T, negative_slope=ALPHA)
        masked = jnp.where(A > 0, e, NEG)
        att = jax.nn.softmax(masked, axis=1)
        H_out = att @ H
        return H_out
    h = jnp.maximum(_layernorm(x, axis=-1), 0.0)
    x = x + _L0_gnn_ref(h, adj, L0_gnn_u, L0_gnn_W1, L0_gnn_b1, L0_gnn_W2, L0_gnn_b2, L0_gnn_Wg, L0_gnn_bg, L0_gnn_Wn, L0_gnn_bn, L0_gnn_g_in, L0_gnn_b_in, L0_gnn_g_out, L0_gnn_b_out)
    h = jnp.maximum(_layernorm(x, axis=-1), 0.0)
    x = x + _L1_gnn_ref(h, adj, L1_gnn_W, L1_gnn_b, L1_gnn_a_s, L1_gnn_a_r)
    return x

_drawn_inputs = setup_inputs


def setup_inputs(seed=0):
    import zlib

    import numpy as np

    out = dict(_drawn_inputs(seed))
    spreads = {'L0_gnn_b1': (0.0, 0.1),
     'L0_gnn_b2': (0.0, 0.1),
     'L0_gnn_bg': (0.0, 0.508),
     'L0_gnn_bn': (0.0, 0.1),
     'L0_gnn_g_in': (1.0, 0.2),
     'L0_gnn_b_in': (0.0, 0.1),
     'L0_gnn_g_out': (1.0, 0.2),
     'L0_gnn_b_out': (0.0, 0.1),
     'L1_gnn_b': (0.0, 0.1)}
    factors = {}
    for name, (base, spread) in spreads.items():
        noise = np.random.default_rng([zlib.crc32(name.encode()), seed]).standard_normal(out[name].shape)
        drawn = base * np.exp(spread * noise) if base else spread * noise
        out[name] = jnp.asarray(drawn.astype(out[name].dtype))
    for name, factor in factors.items():
        out[name] = (out[name] * factor).astype(out[name].dtype)
    return out
```

```python
from contextlib import ExitStack

import concourse.bass as bass
from concourse import mybir

F32 = mybir.dt.float32
BF16 = mybir.dt.bfloat16
U8 = mybir.dt.uint8
ALU = mybir.AluOpType
ACT = mybir.ActivationFunctionType
AX = mybir.AxisListType

P = 128
BANK = 512
U_FLOOR = 1e-10
LN_EPS = 1e-5
NEG = -9000000000000000.0
LOWEST = -3.0e38
SLOPE = 0.2
TABLES = "natural_log_exp_and_others"


class Steps:

    def __init__(self, sem, names):
        self.sem, self.names = sem, list(names)
        assert len(set(self.names)) == len(self.names)

    def at(self, n, name):
        return n * len(self.names) + self.names.index(name) + 1

    def all(self, rounds):
        return rounds * len(self.names)


def ln_vector_steps(tag):
    return [f"{s}_{tag}" for s in ("sum", "mean", "center", "power", "var", "seed2", "seed2var", "fix", "rstd")]


def ln_scalar_steps(tag):
    return [f"{s}_{tag}" for s in ("square", "log", "seed")]


def per_tile(stat, width):
    return stat.unsqueeze(2).broadcast_to([stat.shape[0], stat.shape[1], width])


def per_column(row, tiles):
    return row.unsqueeze(1).broadcast_to([row.shape[0], tiles, row.shape[1]])


def build(nc, x, adj, u, W1, b1, W2, b2, Wg, bg, Wn, bn, g_in, b_in, g_out, b_out, W, b, a_s, a_r, out):
    N, D = x.shape
    NT = N // P
    GT = 4
    NG = NT // GT
    CW = 1024
    NC = N // CW
    SLOTS0 = 3
    UB = 2
    UC = CW // P // UB
    UG = NC * UC
    PW = GT * P
    PTL = CW // P
    NP = NT // PTL
    HALF = N // 2
    SLOTS1 = 4
    VB = 6
    VU = NT // VB
    NQ = NT // 2
    NI = NT // SLOTS1
    assert D == P and NC % SLOTS0 == 0 and UG % 2 == 0 and NP == NC and VU == 8 and NC * CW == N

    with ExitStack() as ctx:
        def sb(name, shape, dt=F32):
            return ctx.enter_context(nc.sbuf_tensor(name, shape, dt))

        def sem(name):
            return ctx.enter_context(nc.semaphore(name))

        stage = sb("stage", [P, SLOTS1 * N])
        work = sb("work", [P, 11264])
        feats = sb("feats", [P, NT, D])
        r_row = sb("r_row", [P, N])
        s_col = sb("s_col", [P, NT])
        r_col = sb("r_col", [P, GT])
        gate = sb("gate", [P, NT])
        ident = sb("ident", [P, P])
        wcat = sb("wcat", [P, 2, 2 * P])
        wn_sb = sb("wn_sb", [P, 2])
        wT = sb("wT", [P, P])
        wraw = sb("wraw", [P, P])
        bcat = sb("bcat", [P, 2 * P])
        rows = sb("rows", [P, 7, P])
        ROW = {n: rows[:, i, :] for i, n in enumerate(("b2", "g_in", "b_in", "g_out", "b_out", "b", "a_s"))}
        ar_row = sb("ar_row", [P, P])
        bn_row = sb("bn_row", [P, 2])
        noise = sb("noise", [P, NT, 2])
        lstat = sb("lstat", [P, 10, PTL])
        zbuf = sb("zbuf", [P, 2, PTL, 2])
        zstat = sb("zstat", [P, 6, PTL])
        eps = sb("eps", [P, 2])

        ring = [stage[:, s * GT * CW:(s + 1) * GT * CW].rearrange("p (t c) -> p t c", t=GT) for s in range(SLOTS0)]
        xg0 = SLOTS0 * GT * CW
        gated = stage[:, xg0:xg0 + NT * D].rearrange("p (t d) -> p t d", t=NT)
        e0 = xg0 + NT * D
        carry_in = stage[:, e0:e0 + GT * 3 * P].rearrange("p (t d) -> p t d", t=GT)
        e0 += GT * 3 * P

        def epi(i):
            return stage[:, e0 + i * PW:e0 + (i + 1) * PW]

        def tiles(a, n=GT):
            return a.rearrange("p (t d) -> p t d", t=n)

        x_in, rawT, fg, v2, dlt, y, sq, h1, h1T = (epi(i) for i in range(9))
        assert e0 + 9 * PW <= SLOTS1 * N
        turned = [work[:, i * UB * PW:(i + 1) * UB * PW] for i in range(2)]
        w0 = 2 * UB * PW
        PX = PTL * D

        def piece(i, n=1):
            return work[:, w0 + i * PX:w0 + (i + n) * PX]

        x8 = [piece(0), piece(1)]
        c8, sq8, xn8, xnT8 = piece(2), piece(3), piece(4), piece(5)
        carry8 = piece(6, 3).rearrange("p (t d) -> p t d", t=PTL)
        assert w0 + 9 * PX <= 11264
        slot = [stage[:, s * N:(s + 1) * N] for s in range(SLOTS1)]
        mbias = [work[:, i * HALF // 2:(i + 1) * HALF // 2].bitcast(BF16) for i in range(2)]
        p0 = HALF
        probT = [work[:, p0 + i * VB * 2 * P:p0 + (i + 1) * VB * 2 * P] for i in range(2)]
        assert p0 + 4 * VB * P <= 11264
        maxes = sb("maxes", [P, 2])
        negmax = sb("negmax", [P, SLOTS1])
        sums = sb("sums", [P, SLOTS1, 2])
        rinv = sb("rinv", [P, 2])
        oT = sb("oT", [P, 2 * P])
        x1_in = sb("x1_in", [P, 2, P])
        fin = sb("fin", [P, 2, P])

        psum = ctx.enter_context(nc.psum_tensor("psum", [P, 8 * BANK], F32))

        def bank(i, n=1):
            return psum[:, i * BANK:(i + n) * BANK]

        turning0 = [bank(0, 2), bank(2, 2)]
        acc0 = bank(4)
        ep = [bank(5), bank(6), bank(7)]
        turning1 = [bank(0, 3), bank(3, 3)]
        acc1 = [bank(6)[:, 0:2 * P], bank(7)[:, 0:2 * P]]
        final = [bank(6)[:, 2 * P:4 * P], bank(7)[:, 2 * P:4 * P]]

        carry = nc.dram_tensor("carry", (N, 3 * P), F32, kind="Internal").ap()
        x_mid = nc.dram_tensor("x_mid", (N, D), F32, kind="Internal").ap()

        def by_tile(a):
            return a.rearrange("(t p) d -> p t d", p=P)

        consts_in = sem("consts_in")
        noise_in = sem("noise_in")
        x_loaded = [sem("x_loaded0"), sem("x_loaded1")]
        ident_ready = sem("ident_ready")
        noise_vec = Steps(sem("noise_vec"), ["eps_log", "eps_ln", "clipped", "bias"])
        noise_act = Steps(sem("noise_act"), ["log", "loglog"])
        wT_turned, wT_ready = sem("wT_turned"), sem("wT_ready")
        piece_vec = Steps(sem("piece_vec"), [
            *ln_vector_steps("x"), "h", *ln_vector_steps("h"), "normed", "scaled", "xn",
            "z", "zmax", "zsub", "esum", "erec", "p1", "hard", "y", "gate", "gated", "mix0", "mix1", "mix2", "mix3"])
        piece_act = Steps(sem("piece_act"), [*ln_scalar_steps("x"), *ln_scalar_steps("h"), "xnT0", "xnT1", "exp"])
        piece_pe = Steps(sem("piece_pe"), ["turn0", "turn1", "logits", "mix0", "mix1", "mix2", "mix3"])
        carry_stored = sem("carry_stored")
        chunk_full = [sem(f"chunk_full{s}") for s in range(SLOTS0)]
        blocks_turned = sem("blocks_turned")
        turned_ready = [sem("turned_ready0"), sem("turned_ready1")]
        unit_summed = sem("unit_summed")
        acc_copied = sem("acc_copied")
        epi_vec = Steps(sem("epi_vec"), [
            *(f"gpre{t}" for t in range(GT)), *(f"view2_{t}" for t in range(GT)),
            "gap", "one_plus", "sigmoid", "mixed", "fused", "resid",
            *ln_vector_steps("out"), "normed", "scaled", "shifted", "x_mid",
            *ln_vector_steps("next"), "h1", "H", "Hs", "s", "Hr", "r", "r_wide"])
        epi_act = Steps(sem("epi_act"), ["exp", *ln_scalar_steps("out"), *ln_scalar_steps("next"), "h1T", "r_row"])
        epi_pe = Steps(sem("epi_pe"), ["mix01", "mix23", "turn", "H", "r_row"])
        carry_loaded = sem("carry_loaded")
        x_mid_stored = sem("x_mid_stored")
        half_full = [[sem(f"half_full{s}_{c}") for c in range(2)] for s in range(SLOTS1)]
        leaky_ready = sem("leaky_ready")
        mask_ready = sem("mask_ready")
        product_ready = sem("product_ready")
        half_max = sem("half_max")
        max_ready = sem("max_ready")
        exp_done = sem("exp_done")
        probs_turned = sem("probs_turned")
        probT_ready = [sem("probT_ready0"), sem("probT_ready1")]
        probs_summed = sem("probs_summed")
        fin_vec = Steps(sem("fin_vec"), ["oT", "total", "rinv", "scaled", "out"])
        fin_turned = sem("fin_turned")
        xm_loaded = sem("xm_loaded")
        out_stored = sem("out_stored")

        waits_met = sem("waits_met")

        def met(engine):
            engine.sem_inc(waits_met, 1)

        def at_slot(i, s):
            return i + s // SLOTS1, s % SLOTS1

        block = ctx.enter_context(nc.Block())

        @block.sync
        def _(sp):
            def load_piece(n):
                if n >= 2:
                    sp.wait_ge(piece_vec.sem, piece_vec.at(n - 2, "center_x"))
                sp.dma_start(tiles(x8[n % 2], PTL), by_tile(x)[:, n * PTL:(n + 1) * PTL, :]).then_inc(x_loaded[n % 2], 16)

            def store_carry(n):
                sp.wait_ge(piece_vec.sem, piece_vec.at(n, "mix3"))
                sp.dma_start(by_tile(carry)[:, n * PTL:(n + 1) * PTL, :], carry8).then_inc(carry_stored, 16)

            adj_groups = adj.rearrange("(g t p) c -> g p t c", t=GT, p=P)

            def load_chunk(g, c, first):
                s = c % SLOTS0
                if not (first and c < SLOTS0):
                    sp.wait_ge(blocks_turned, g * UG + (c - SLOTS0 + 1) * UC)
                sp.dma_start(ring[s], adj_groups[g, :, :, c * CW:(c + 1) * CW]).then_inc(chunk_full[s], 16)

            def load_carry(g):
                sp.wait_ge(x_mid_stored, 16 * g)
                fetch_carry(g)

            def fetch_carry(g):
                sp.dma_start(carry_in, by_tile(carry)[:, bass.ts(g, GT), :]).then_inc(carry_loaded, 16)
                sp.dma_start(tiles(x_in), by_tile(x)[:, bass.ts(g, GT), :]).then_inc(carry_loaded, 16)

            def store_x_mid(g):
                sp.wait_ge(epi_vec.sem, epi_vec.at(g, "x_mid"))
                sp.dma_start(by_tile(x_mid)[:, bass.ts(g, GT), :], tiles(y)).then_inc(x_mid_stored, 16)

            load_piece(0)
            for src, dst in ((u.rearrange("(t p) k -> p t k", p=P), noise[:]),
                             (bn.partition_broadcast(P), bn_row[:])):
                sp.dma_start(dst, src).then_inc(noise_in, 16)
            for src, dst in ((Wg[0:P, :], wcat[:, 0, 0:P]), (W1, wcat[:, 0, P:2 * P]),
                             (Wg[P:2 * P, :], wcat[:, 1, 0:P]), (W2, wcat[:, 1, P:2 * P]),
                             (Wn, wn_sb[:]), (W, wraw[:]),
                             (bg.partition_broadcast(P), bcat[:, 0:P]), (b1.partition_broadcast(P), bcat[:, P:2 * P]),
                             (b2.partition_broadcast(P), ROW["b2"]), (g_in.partition_broadcast(P), ROW["g_in"]),
                             (b_in.partition_broadcast(P), ROW["b_in"]), (g_out.partition_broadcast(P), ROW["g_out"]),
                             (b_out.partition_broadcast(P), ROW["b_out"]), (b.partition_broadcast(P), ROW["b"]),
                             (a_s.rearrange("d k -> (k d)").partition_broadcast(P), ROW["a_s"]),
                             (a_r.rearrange("d k -> (k d)").partition_broadcast(P), ar_row[:])):
                sp.dma_start(dst, src).then_inc(consts_in, 16)
            load_piece(1)
            for c in range(SLOTS0):
                load_chunk(0, c, True)
            for n in range(2, NP):
                load_piece(n)
                store_carry(n - 2)
                if n - 2 + SLOTS0 < NC:
                    load_chunk(0, n - 2 + SLOTS0, True)
            store_carry(NP - 2)
            store_carry(NP - 1)
            sp.wait_ge(carry_stored, 16 * NP)
            fetch_carry(0)
            with sp.Fori(1, NG) as g:
                for c in range(NC):
                    load_chunk(g, c, False)
                store_x_mid(g - 1)
                load_carry(g)
            store_x_mid(NG - 1)

            adj_tiles = adj.rearrange("(t p) c -> t p c", p=P)

            def load_half(k, s, c):
                sp.dma_start(slot[s][:, c * HALF:(c + 1) * HALF],
                             adj_tiles[k, :, c * HALF:(c + 1) * HALF]).then_inc(half_full[s][c], 16)

            for s in range(SLOTS1):
                if s == 0:
                    sp.wait_ge(blocks_turned, NG * UG)
                if s == 2:
                    sp.wait_ge(unit_summed, NG * UG)
                    sp.wait_ge(epi_vec.sem, epi_vec.all(NG))
                    sp.wait_ge(epi_act.sem, epi_act.all(NG))
                    sp.wait_ge(epi_pe.sem, epi_pe.all(NG))
                    sp.wait_ge(x_mid_stored, 16 * NG)
                for c in range(2):
                    load_half(s, s, c)
            with sp.Fori(1, NI) as i:
                for q in range(2):
                    for c in range(2):
                        sp.wait_ge(probs_turned, (2 * i + q - 2) * VU + (c + 1) * (VU // 2))
                        for s in (2 * q, 2 * q + 1):
                            load_half(SLOTS1 * i + s, s, c)

        @block.gpsimd
        def _(pool):
            pool.memset(ident[:], 0.0).then_inc(ident_ready, 1)
            pool.wait_ge(ident_ready, 1)
            pool.affine_select(out=ident[:], in_=ident[:], compare_op=ALU.not_equal, fill=1.0, base=0,
                               pattern=[[-1, P]], channel_multiplier=1).then_inc(ident_ready, 1)
            pool.wait_ge(x_mid_stored, 16 * NG)

            def finish(q):
                pool.dma_start(x1_in[:], by_tile(x_mid)[:, bass.ts(q, 2), :]).then_inc(xm_loaded, 16)
                pool.wait_ge(fin_vec.sem, fin_vec.at(q, "out"))
                met(pool)
                pool.dma_start(by_tile(out)[:, bass.ts(q, 2), :], fin[:]).then_inc(out_stored, 16)
                pool.wait_ge(out_stored, 16 * (q + 1))

            with pool.Fori(0, NQ) as q:
                finish(q)

        @block.scalar
        def _(act):
            def ln_scalar(steps, vec, n, tag, src, dst, stat):
                act.wait_ge(vec.sem, vec.at(n, f"center_{tag}"))
                act.activation(dst, src, ACT.Square).then_inc(steps.sem, 1)
                act.wait_ge(vec.sem, vec.at(n, f"power_{tag}"))
                act.activation(stat[3], stat[2], ACT.Ln, scale=1.0 / D, bias=eps[:, 0:1]).then_inc(steps.sem, 1)
                act.wait_ge(steps.sem, steps.at(n, f"log_{tag}"))
                act.activation(stat[4], stat[3], ACT.Exp, scale=-0.5).then_inc(steps.sem, 1)

            act.preload_act_table_set(TABLES)
            act.wait_ge(noise_vec.sem, noise_vec.at(0, "clipped"))
            act.activation(noise[:], noise[:], ACT.Ln).then_inc(noise_act.sem, 1)
            act.wait_ge(noise_act.sem, noise_act.at(0, "log"))
            act.activation(noise[:], noise[:], ACT.Ln, scale=-1.0, bias=eps[:, 1:2]).then_inc(noise_act.sem, 1)

            def piece_steps(n):
                st = [lstat[:, i, :] for i in range(10)]

                def norms_x():
                    ln_scalar(piece_act, piece_vec, n, "x", c8, sq8, st)

                def norms_h():
                    ln_scalar(piece_act, piece_vec, n, "h", c8, sq8, st)

                def copies():
                    for i in range(2):
                        act.wait_ge(piece_pe.sem, piece_pe.at(n, f"turn{i}"))
                        act.activation(xnT8[:, i * BANK:(i + 1) * BANK], ep[i], ACT.Copy).then_inc(piece_act.sem, 1)

                def exps():
                    act.wait_ge(piece_vec.sem, piece_vec.at(n, "zsub"))
                    act.activation(zbuf[:, 1], zbuf[:, 0], ACT.Exp).then_inc(piece_act.sem, 1)
                return [norms_x, norms_h, copies, exps]

            def evacuate(g, v, first):
                n = g * UG + v
                act.wait_ge(blocks_turned, n + 1)
                if not (first and v < 2):
                    act.wait_ge(unit_summed, n - 1)
                act.activation(turned[v % 2], turning0[v % 2], ACT.Copy).then_inc(turned_ready[v % 2], 1)

            def copy_acc(g):
                act.wait_ge(unit_summed, (g + 1) * UG)
                act.activation(rawT, acc0, ACT.Copy).then_inc(acc_copied, 1)

            estat = [lstat[:, i, 0:GT] for i in range(10)]

            def epi_exp(g):
                act.wait_ge(epi_vec.sem, epi_vec.at(g, f"view2_{GT - 1}"))
                act.activation(fg, fg, ACT.Exp, scale=-1.0).then_inc(epi_act.sem, 1)

            def epi_turn(g):
                act.wait_ge(epi_pe.sem, epi_pe.at(g, "turn"))
                act.activation(h1T, ep[2], ACT.Copy).then_inc(epi_act.sem, 1)

            def epi_r(g):
                act.wait_ge(epi_pe.sem, epi_pe.at(g, "r_row"))
                act.activation(r_row[:, bass.ts(g, PW)], ep[1], ACT.Copy).then_inc(epi_act.sem, 1)

            def epilogue(g):
                return {1: [lambda: epi_exp(g)],
                        5: [lambda: ln_scalar(epi_act, epi_vec, g, "out", dlt, sq, estat)],
                        11: [lambda: ln_scalar(epi_act, epi_vec, g, "next", dlt, sq, estat)],
                        15: [lambda: epi_turn(g)],
                        21: [lambda: epi_r(g)]}

            for f in piece_steps(0):
                f()
            for c in range(NC):
                nxt = piece_steps(c + 1) if c + 1 < NP else []
                for w in range(UC):
                    if w < len(nxt):
                        nxt[w]()
                    evacuate(0, c * UC + w, True)
            with act.Fori(1, NG) as g:
                todo = epilogue(g - 1)
                for v in range(UG):
                    if v % 2 == 0:
                        evacuate(g, v, False)
                    if v == 0:
                        copy_acc(g - 1)
                    for f in todo.get(v, []):
                        f()
            copy_acc(NG - 1)
            for fs in epilogue(NG - 1).values():
                for f in fs:
                    f()

            def exps(i, s, c, first):
                i, s = at_slot(i, s)
                act.wait_ge(max_ready, SLOTS1 * i + s + 1)
                if c == 0 and not first:
                    act.wait_ge(fin_vec.sem, fin_vec.at(2 * i + s // 2 - 2, "total"))
                half = slot[s][:, c * HALF:(c + 1) * HALF]
                act.activation(half, half, ACT.Exp, bias=negmax[:, s:s + 1],
                               accum_out=sums[:, s, c:c + 1]).then_inc(exp_done, 1)

            def evacuate1(i, s, v, first):
                i, s = at_slot(i, s)
                n = (2 * i + s // 2) * VU + v
                act.wait_ge(probs_turned, n + 1)
                if not (first and v < 2):
                    act.wait_ge(probs_summed, n - 1)
                act.activation(probT[v % 2], turning1[v % 2], ACT.Copy).then_inc(probT_ready[v % 2], 1)

            def step(i, s, start=False, fresh=False):
                quarter = VU // 2 * (s % 2)
                for c in range(2):
                    if not (start and s == 0):
                        exps(i, s - 1, c, start or fresh)
                    if not (start and s < 2):
                        for v in (quarter + 2 * c, quarter + 2 * c + 1):
                            evacuate1(i, s - 2, v, start and s == 2)

            for s in range(1, SLOTS1):
                step(0, s, start=True)
            step(1, 0, fresh=True)
            with act.Fori(1, NI - 1) as i:
                for s in range(1, SLOTS1 + 1):
                    step(*at_slot(i, s))
            for s in range(1, SLOTS1 + 1):
                step(NI - 1, s) if s < SLOTS1 else step(NI, 0)
            for v in range(VU // 2, VU):
                evacuate1(NI - 1, 2, v, False)

        @block.tensor
        def _(pe):
            pe.wait_ge(ident_ready, 2)
            pe.wait_ge(consts_in, 16 * 16)
            pe.transpose(ep[2][:, P:2 * P], wraw[:], ident[:]).then_inc(wT_turned, 1)

            def piece_turn(n):
                pe.wait_ge(piece_vec.sem, piece_vec.at(n, "xn"))
                for i in range(2):
                    if n >= 1:
                        pe.wait_ge(piece_vec.sem, piece_vec.at(n - 1, f"mix{2 + i}"))
                    for t in range(4):
                        mm = pe.transpose(ep[i][:, t * P:(t + 1) * P], tiles(xn8, PTL)[:, 4 * i + t, :], ident[:])
                    mm.then_inc(piece_pe.sem, 1)

            def piece_logits(n):
                if n == 0:
                    pe.wait_ge(wT_ready, 1)
                pe.wait_ge(piece_act.sem, piece_act.at(n, "xnT1"))
                for t in range(PTL):
                    mm = pe.matmul(ep[2][:, 2 * t:2 * t + 2], xnT8[:, t * P:(t + 1) * P], wn_sb[:], start=True, stop=True)
                mm.then_inc(piece_pe.sem, 1)

            def piece_mix(n):
                for i in range(4):
                    if i >= 2:
                        pe.wait_ge(piece_vec.sem, piece_vec.at(n, f"mix{i - 2}"))
                    for t in range(2):
                        mm = pe.matmul(ep[i % 2][:, t * 2 * P:(t + 1) * 2 * P], xnT8[:, (2 * i + t) * P:(2 * i + t + 1) * P],
                                       wcat[:, 0, :], start=True, stop=True)
                    mm.then_inc(piece_pe.sem, 1)

            def turn(g, v, first):
                n = g * UG + v
                c, w = v // UC, v % UC
                s = c % SLOTS0
                if w == 0:
                    pe.wait_ge(chunk_full[s], 16 * (g * (NC // SLOTS0) + c // SLOTS0 + 1))
                if not (first and v < 2):
                    pe.wait_ge(turned_ready[v % 2], g * (UG // 2) + v // 2)
                for j in range(UB):
                    for t in range(GT):
                        mm = pe.transpose(turning0[v % 2][:, j * PW + t * P:j * PW + (t + 1) * P],
                                          ring[s][:, t, (w * UB + j) * P:(w * UB + j + 1) * P], ident[:])
                mm.then_inc(blocks_turned, 1)

            def gather(g, v, first):
                if first and v % UC == 0:
                    pe.wait_ge(piece_vec.sem, piece_vec.at(v // UC, "gated"))
                if v == 0 and not first:
                    pe.wait_ge(acc_copied, g)
                pe.wait_ge(turned_ready[v % 2], g * (UG // 2) + v // 2 + 1)
                for j in range(UB):
                    blk = v * UB + j
                    mm = pe.matmul(acc0, gated[:, blk, :], turned[v % 2][:, j * PW:(j + 1) * PW],
                                   start=blk == 0, stop=blk == NT - 1)
                mm.then_inc(unit_summed, 1)

            def epi_mix(g, i):
                if i == 0:
                    pe.wait_ge(acc_copied, g + 1)
                    pe.wait_ge(piece_vec.sem, piece_vec.all(NP))
                for t in range(2):
                    mm = pe.matmul(ep[i][:, t * 2 * P:(t + 1) * 2 * P], rawT[:, (2 * i + t) * P:(2 * i + t + 1) * P],
                                   wcat[:, 1, :], start=True, stop=True)
                mm.then_inc(epi_pe.sem, 1)

            def epi_turn(g):
                pe.wait_ge(epi_vec.sem, epi_vec.at(g, "h1"))
                for t in range(GT):
                    mm = pe.transpose(ep[2][:, t * P:(t + 1) * P], h1[:, t * P:(t + 1) * P], ident[:])
                mm.then_inc(epi_pe.sem, 1)

            def epi_h(g):
                pe.wait_ge(epi_act.sem, epi_act.at(g, "h1T"))
                for t in range(GT):
                    mm = pe.matmul(ep[0][:, t * P:(t + 1) * P], h1T[:, t * P:(t + 1) * P], wT[:], start=True, stop=True)
                mm.then_inc(epi_pe.sem, 1)

            def epi_r(g):
                pe.wait_ge(epi_vec.sem, epi_vec.at(g, "r_wide"))
                for t in range(GT):
                    mm = pe.matmul(ep[1][:, t * P:(t + 1) * P], dlt[:, t * P:(t + 1) * P], ident[:], start=True, stop=True)
                mm.then_inc(epi_pe.sem, 1)

            def epilogue(g):
                return {0: [lambda: epi_mix(g, 0), lambda: epi_mix(g, 1)], 14: [lambda: epi_turn(g)],
                        16: [lambda: epi_h(g)], 20: [lambda: epi_r(g)]}

            piece_turn(0)
            piece_logits(0)
            piece_mix(0)
            for v in range(UG):
                c, w = v // UC, v % UC
                turn(0, v, True)
                if v >= 1:
                    gather(0, v - 1, True)
                if c + 1 < NP and w < 3:
                    (piece_turn, piece_logits, piece_mix)[w](c + 1)
            with pe.Fori(1, NG) as g:
                todo = epilogue(g - 1)
                for v in range(UG):
                    turn(g, v, False)
                    if v == 0:
                        gather(g - 1, UG - 1, False)
                    else:
                        gather(g, v - 1, False)
                    for f in todo.get(v - 1, []):
                        f()
            gather(NG - 1, UG - 1, False)
            for fs in epilogue(NG - 1).values():
                for f in fs:
                    f()

            def turn1(q, qs, v, first):
                c = v // (VU // 2)
                if v % (VU // 2) == 0:
                    pe.wait_ge(exp_done, 2 * (2 * q + 1) + c + 1)
                if not (first and v < 2):
                    pe.wait_ge(probT_ready[v % 2], q * (VU // 2) + v // 2)
                for j in range(VB):
                    for t in range(2):
                        mm = pe.transpose(turning1[v % 2][:, (2 * j + t) * P:(2 * j + t + 1) * P],
                                          slot[2 * qs + t][:, (v * VB + j) * P:(v * VB + j + 1) * P], ident[:])
                mm.then_inc(probs_turned, 1)

            def gather1(q, qs, v):
                pe.wait_ge(probT_ready[v % 2], q * (VU // 2) + v // 2 + 1)
                for j in range(VB):
                    blk = v * VB + j
                    mm = pe.matmul(acc1[qs], feats[:, blk, :], probT[v % 2][:, j * 2 * P:(j + 1) * 2 * P],
                                   start=blk == 0, stop=blk == NT - 1)
                mm.then_inc(probs_summed, 1)

            def turn_sums(q, qs):
                pe.wait_ge(fin_vec.sem, fin_vec.at(q, "oT"))
                for t in range(2):
                    mm = pe.transpose(final[qs][:, t * P:(t + 1) * P], oT[:, t * P:(t + 1) * P], ident[:])
                mm.then_inc(fin_turned, 1)

            def pair(q, qs, first):
                for v in range(VU):
                    turn1(q, qs, v, first)
                    if v == 0 and not first:
                        gather1(q - 1, 1 - qs, VU - 1)
                    if v >= 1:
                        gather1(q, qs, v - 1)
                    if v == 2 and not first:
                        turn_sums(q - 1, 1 - qs)

            pe.wait_ge(epi_vec.sem, epi_vec.all(NG))
            pe.wait_ge(epi_act.sem, epi_act.all(NG))
            pair(0, 0, True)
            pair(1, 1, False)
            with pe.Fori(1, NI) as i:
                pair(2 * i, 0, False)
                pair(2 * i + 1, 1, False)
            gather1(NQ - 1, 1, VU - 1)
            turn_sums(NQ - 1, 1)

        @block.vector
        def _(vec):
            def ln_vector(steps, acts, n, tag, src, center, sq_, stat, tl, ready=None):
                ssum, nmean, power, _, seed, var, s2, s2v, fix, rstd = stat

                def done(name):
                    vec.wait_ge(steps.sem, steps.at(n, name))

                vec.tensor_reduce(ssum, src, AX.X, ALU.add).then_inc(steps.sem, 1)
                done(f"sum_{tag}")
                vec.tensor_scalar(nmean, ssum, -1.0 / D, None, ALU.mult).then_inc(steps.sem, 1)
                done(f"mean_{tag}")
                vec.tensor_tensor(tiles(center, tl), src, per_tile(nmean, D), ALU.add).then_inc(steps.sem, 1)
                vec.wait_ge(acts.sem, acts.at(n, f"square_{tag}"))
                vec.tensor_reduce(power, tiles(sq_, tl), AX.X, ALU.add).then_inc(steps.sem, 1)
                done(f"power_{tag}")
                vec.tensor_scalar(var, power, 1.0 / D, LN_EPS, ALU.mult, ALU.add).then_inc(steps.sem, 1)
                vec.wait_ge(acts.sem, acts.at(n, f"seed_{tag}"))
                vec.tensor_tensor(s2, seed, seed, ALU.mult).then_inc(steps.sem, 1)
                done(f"seed2_{tag}")
                vec.tensor_tensor(s2v, s2, var, ALU.mult).then_inc(steps.sem, 1)
                done(f"seed2var_{tag}")
                vec.tensor_scalar(fix, s2v, -0.5, 1.5, ALU.mult, ALU.add).then_inc(steps.sem, 1)
                done(f"fix_{tag}")
                vec.tensor_tensor(rstd, seed, fix, ALU.mult).then_inc(steps.sem, 1)
                done(f"rstd_{tag}")

            vec.memset(eps[:, 0:1], LN_EPS).then_inc(noise_vec.sem, 1)
            vec.memset(eps[:, 1:2], U_FLOOR).then_inc(noise_vec.sem, 1)
            vec.wait_ge(noise_in, 32)
            vec.tensor_scalar(noise[:], noise[:], U_FLOOR, 1.0, ALU.max, ALU.min).then_inc(noise_vec.sem, 1)
            vec.wait_ge(noise_act.sem, noise_act.at(0, "loglog"))
            vec.tensor_tensor(noise[:], per_column(bn_row[:], NT), noise[:], ALU.subtract).then_inc(noise_vec.sem, 1)

            def do_piece(n):
                ps = piece_vec
                st = [lstat[:, i, :] for i in range(10)]

                def done(name):
                    vec.wait_ge(ps.sem, ps.at(n, name))

                vec.wait_ge(x_loaded[n % 2], 16 * (n // 2 + 1))
                ln_vector(ps, piece_act, n, "x", tiles(x8[n % 2], PTL), c8, sq8, st, PTL)
                if n >= 1:
                    vec.wait_ge(carry_stored, 16 * n)
                h8 = carry8[:, :, 2 * P:3 * P]
                vec.scalar_tensor_tensor(h8, tiles(c8, PTL), 0.0, per_tile(st[9], D), ALU.max, ALU.mult).then_inc(ps.sem, 1)
                done("h")
                ln_vector(ps, piece_act, n, "h", h8, c8, sq8, st, PTL)
                vec.tensor_tensor(tiles(xn8, PTL), tiles(c8, PTL), per_tile(st[9], D), ALU.mult).then_inc(ps.sem, 1)
                done("normed")
                if n == 0:
                    vec.wait_ge(consts_in, 16 * 16)
                vec.tensor_tensor(tiles(xn8, PTL), tiles(xn8, PTL), per_column(ROW["g_in"], PTL), ALU.mult).then_inc(ps.sem, 1)
                done("scaled")
                vec.tensor_tensor(tiles(xn8, PTL), tiles(xn8, PTL), per_column(ROW["b_in"], PTL), ALU.add).then_inc(ps.sem, 1)
                if n == 0:
                    vec.wait_ge(wT_turned, 1)
                    vec.tensor_copy(wT[:], ep[2][:, P:2 * P]).then_inc(wT_ready, 1)
                    vec.wait_ge(noise_vec.sem, noise_vec.at(0, "bias"))
                z, e = zbuf[:, 0], zbuf[:, 1]
                zmax, esum, erec, p1, hard, ysum = (zstat[:, i, :] for i in range(6))
                vec.wait_ge(piece_pe.sem, piece_pe.at(n, "logits"))
                vec.tensor_tensor(z, ep[2][:, 0:2 * PTL].rearrange("p (t k) -> p t k", k=2),
                                  noise[:, n * PTL:(n + 1) * PTL, :], ALU.add).then_inc(ps.sem, 1)
                done("z")
                vec.tensor_tensor(zmax, z[:, :, 0], z[:, :, 1], ALU.max).then_inc(ps.sem, 1)
                done("zmax")
                vec.tensor_tensor(z, z, per_tile(zmax, 2), ALU.subtract).then_inc(ps.sem, 1)
                vec.wait_ge(piece_act.sem, piece_act.at(n, "exp"))
                vec.tensor_tensor(esum, e[:, :, 0], e[:, :, 1], ALU.add).then_inc(ps.sem, 1)
                done("esum")
                vec.reciprocal(erec, esum).then_inc(ps.sem, 1)
                done("erec")
                vec.tensor_tensor(p1, e[:, :, 1], erec, ALU.mult).then_inc(ps.sem, 1)
                vec.tensor_tensor(hard, z[:, :, 1], z[:, :, 0], ALU.is_gt).then_inc(ps.sem, 1)
                done("hard")
                vec.tensor_tensor(ysum, hard, p1, ALU.add).then_inc(ps.sem, 1)
                done("y")
                vec.tensor_tensor(gate[:, n * PTL:(n + 1) * PTL], ysum, p1, ALU.subtract).then_inc(ps.sem, 1)
                done("gate")
                vec.tensor_tensor(gated[:, n * PTL:(n + 1) * PTL, :], tiles(xn8, PTL),
                                  per_tile(gate[:, n * PTL:(n + 1) * PTL], D), ALU.mult).then_inc(ps.sem, 1)
                for i in range(4):
                    vec.wait_ge(piece_pe.sem, piece_pe.at(n, f"mix{i}"))
                    vec.tensor_tensor(carry8[:, 2 * i:2 * i + 2, 0:2 * P], tiles(ep[i % 2], 2),
                                      per_column(bcat[:], 2), ALU.add).then_inc(ps.sem, 1)

            def evacuate(g, v):
                n = g * UG + v
                vec.wait_ge(blocks_turned, n + 1)
                vec.wait_ge(unit_summed, n - 1)
                vec.tensor_copy(turned[v % 2], turning0[v % 2]).then_inc(turned_ready[v % 2], 1)

            estat = [lstat[:, i, 0:GT] for i in range(10)]
            v1 = carry_in[:, :, P:2 * P]
            hres = carry_in[:, :, 2 * P:3 * P]

            def epi_view2(g):
                es = epi_vec
                vec.wait_ge(carry_loaded, 32 * (g + 1))
                for t in range(GT):
                    if t % 2 == 0:
                        vec.wait_ge(epi_pe.sem, epi_pe.at(g, ("mix01", "mix23")[t // 2]))
                    ps = ep[t // 2][:, (t % 2) * 2 * P:(t % 2) * 2 * P + P]
                    vec.scalar_tensor_tensor(tiles(fg)[:, t, :], ps, gate[:, bass.ds(g * GT + t, 1)],
                                             carry_in[:, t, 0:P], ALU.mult, ALU.add).then_inc(es.sem, 1)
                for t in range(GT):
                    ps = ep[t // 2][:, (t % 2) * 2 * P + P:(t % 2 + 1) * 2 * P]
                    vec.scalar_tensor_tensor(tiles(v2)[:, t, :], ps, gate[:, bass.ds(g * GT + t, 1)],
                                             ROW["b2"], ALU.mult, ALU.add).then_inc(es.sem, 1)

            def epi_fuse(g):
                es = epi_vec

                def done(name):
                    vec.wait_ge(es.sem, es.at(g, name))

                done(f"view2_{GT - 1}")
                vec.tensor_tensor(tiles(dlt), v1, tiles(v2), ALU.subtract).then_inc(es.sem, 1)
                vec.wait_ge(epi_act.sem, epi_act.at(g, "exp"))
                vec.tensor_scalar(fg, fg, 1.0, None, ALU.add).then_inc(es.sem, 1)
                done("one_plus")
                vec.reciprocal(fg, fg).then_inc(es.sem, 1)
                done("sigmoid")
                vec.tensor_tensor(dlt, dlt, fg, ALU.mult).then_inc(es.sem, 1)

            def epi_resid(g):
                es = epi_vec

                def done(name):
                    vec.wait_ge(es.sem, es.at(g, name))

                done("mixed")
                vec.tensor_tensor(y, v2, dlt, ALU.add).then_inc(es.sem, 1)
                done("fused")
                vec.tensor_tensor(tiles(y), tiles(y), hres, ALU.add).then_inc(es.sem, 1)
                done("resid")

            def epi_norm_out(g):
                ln_vector(epi_vec, epi_act, g, "out", tiles(y), dlt, sq, estat, GT)

            def epi_x_mid(g):
                es = epi_vec

                def done(name):
                    vec.wait_ge(es.sem, es.at(g, name))

                vec.tensor_tensor(tiles(y), tiles(dlt), per_tile(estat[9], D), ALU.mult).then_inc(es.sem, 1)
                done("normed")
                vec.tensor_tensor(tiles(y), tiles(y), per_column(ROW["g_out"], GT), ALU.mult).then_inc(es.sem, 1)
                done("scaled")
                vec.tensor_tensor(tiles(y), tiles(y), per_column(ROW["b_out"], GT), ALU.add).then_inc(es.sem, 1)
                done("shifted")
                vec.tensor_tensor(y, y, x_in, ALU.add).then_inc(es.sem, 1)
                done("x_mid")

            def epi_norm_next(g):
                es = epi_vec
                ln_vector(es, epi_act, g, "next", tiles(y), dlt, sq, estat, GT)
                vec.scalar_tensor_tensor(tiles(h1), tiles(dlt), 0.0, per_tile(estat[9], D),
                                         ALU.max, ALU.mult).then_inc(es.sem, 1)

            def epi_heads(g):
                es = epi_vec

                def done(name):
                    vec.wait_ge(es.sem, es.at(g, name))

                H = feats[:, bass.ts(g, GT), :]
                vec.wait_ge(epi_pe.sem, epi_pe.at(g, "H"))
                vec.tensor_tensor(H, tiles(ep[0]), per_column(ROW["b"], GT), ALU.add).then_inc(es.sem, 1)
                done("H")
                vec.tensor_tensor(tiles(fg), H, per_column(ROW["a_s"], GT), ALU.mult).then_inc(es.sem, 1)
                done("Hs")
                vec.tensor_reduce(s_col[:, bass.ts(g, GT)], tiles(fg), AX.X, ALU.add).then_inc(es.sem, 1)
                vec.tensor_tensor(tiles(v2), H, per_column(ar_row[:], GT), ALU.mult).then_inc(es.sem, 1)
                done("Hr")
                vec.tensor_reduce(r_col[:], tiles(v2), AX.X, ALU.add).then_inc(es.sem, 1)
                done("r")
                vec.tensor_copy(tiles(dlt), per_tile(r_col[:], P)).then_inc(es.sem, 1)

            for n in range(NP):
                do_piece(n)
            with vec.Fori(1, NG) as g:
                h = g - 1
                todo = {2: [epi_view2], 4: [epi_fuse], 6: [epi_resid, epi_norm_out], 10: [epi_x_mid],
                        12: [epi_norm_next], 18: [epi_heads]}
                for v in range(UG):
                    if v % 2 == 1:
                        evacuate(g, v)
                    for f in todo.get(v, ()):
                        f(h)
            epi_view2(NG - 1)
            epi_fuse(NG - 1)
            epi_resid(NG - 1)
            epi_norm_out(NG - 1)
            epi_x_mid(NG - 1)
            epi_norm_next(NG - 1)
            epi_heads(NG - 1)

            def score(i, s, c, first):
                half = slot[s][:, c * HALF:(c + 1) * HALF]
                n = 2 * (SLOTS1 * i + s) + c
                vec.wait_ge(half_full[s][c], 16 * (i + 1))
                if not first:
                    vec.wait_ge(half_max, n - 1)
                vec.tensor_scalar(mbias[c], half, 0.0, NEG, ALU.is_le, ALU.mult).then_inc(mask_ready, 1)
                vec.scalar_tensor_tensor(half, r_row[:, c * HALF:(c + 1) * HALF], s_col[:, bass.ds(SLOTS1 * i + s, 1)],
                                         half, ALU.add, ALU.mult).then_inc(product_ready, 1)
                vec.wait_ge(mask_ready, n + 1)
                vec.wait_ge(product_ready, n + 1)
                vec.scalar_tensor_tensor(half, half, SLOPE, half, ALU.mult, ALU.max).then_inc(leaky_ready, 1)
                vec.wait_ge(leaky_ready, n + 1)
                met(vec)
                vec.tensor_tensor_reduce(half, half, mbias[c], 1.0, LOWEST, ALU.add, ALU.max,
                                         maxes[:, c:c + 1]).then_inc(half_max, 1)

            def row_max(i, s):
                vec.wait_ge(half_max, 2 * (SLOTS1 * i + s) + 2)
                vec.tensor_reduce(negmax[:, s:s + 1], maxes[:], AX.X, ALU.max, negate=True).then_inc(max_ready, 1)

            def copy_sums(q, qs):
                vec.wait_ge(probs_summed, VU * (q + 1))
                vec.tensor_copy(oT[:], acc1[qs]).then_inc(fin_vec.sem, 1)

            def finish(q, qs):
                fv = fin_vec
                vec.wait_ge(exp_done, 4 * (q + 1))
                vec.tensor_reduce(rinv[:], sums[:, 2 * qs:2 * qs + 2, :], AX.X, ALU.add).then_inc(fv.sem, 1)
                vec.wait_ge(fv.sem, fv.at(q, "total"))
                vec.reciprocal(rinv[:], rinv[:]).then_inc(fv.sem, 1)
                vec.wait_ge(fv.sem, fv.at(q, "rinv"))
                vec.wait_ge(fin_turned, q + 1)
                vec.wait_ge(xm_loaded, 16 * (q + 1))
                vec.tensor_tensor(fin[:], tiles(final[qs], 2), per_tile(rinv[:], P), ALU.mult).then_inc(fv.sem, 1)
                vec.wait_ge(fv.sem, fv.at(q, "scaled"))
                vec.tensor_tensor(fin[:], fin[:], x1_in[:], ALU.add).then_inc(fv.sem, 1)

            def step(i, s, first):
                q = 2 * i + s // 2 - 2
                ends = s % 2 == 0 and not first
                score(i, s, 0, first and s == 0)
                if ends:
                    copy_sums(q, s // 2)
                score(i, s, 1, first and s == 0)
                if ends:
                    finish(q, s // 2)
                row_max(i, s)

            vec.wait_ge(epi_act.sem, epi_act.at(NG - 1, "r_row"))
            vec.wait_ge(epi_vec.sem, epi_vec.all(NG))
            vec.wait_ge(unit_summed, NG * UG)
            for s in range(SLOTS1):
                step(0, s, True)
            with vec.Fori(1, NI) as i:
                for s in range(SLOTS1):
                    step(i, s, False)
            for q in (NQ - 2, NQ - 1):
                copy_sums(q, q % 2)
                finish(q, q % 2)


_INS = ['x', 'adj', 'L0_gnn_u', 'L0_gnn_W1', 'L0_gnn_b1', 'L0_gnn_W2', 'L0_gnn_b2', 'L0_gnn_Wg', 'L0_gnn_bg',
        'L0_gnn_Wn', 'L0_gnn_bn', 'L0_gnn_g_in', 'L0_gnn_b_in', 'L0_gnn_g_out', 'L0_gnn_b_out',
        'L1_gnn_W', 'L1_gnn_b', 'L1_gnn_a_s', 'L1_gnn_a_r']


def kernel(**inputs):
    import numpy as _np
    import concourse.bacc as _bacc
    from concourse import mybir as _mybir
    from concourse.bass_utils import run_bass_kernel_spmd as _run

    nc = _bacc.Bacc("TRN2", target_bir_lowering=False, num_devices=1)
    arrays, args = {}, []
    for name in _INS:
        a = _np.ascontiguousarray(inputs[name])
        arrays[f"in_{name}_dram"] = a
        args.append(nc.dram_tensor(f"in_{name}_dram", a.shape, _mybir.dt.from_np(a.dtype), kind="ExternalInput").ap())
    out = nc.dram_tensor("out_dram", inputs["x"].shape, _mybir.dt.float32, kind="ExternalOutput").ap()
    build(nc, *args, out)
    r = _run(nc, [arrays], core_ids=[0])
    return r.results[0]["out_dram"]
```

```python
from contextlib import ExitStack

import concourse.bass as bass
from concourse import mybir

F32 = mybir.dt.float32
F32R = mybir.dt.float32r
U8 = mybir.dt.uint8
ALU = mybir.AluOpType
ACT = mybir.ActivationFunctionType
AX = mybir.AxisListType

P = 128
BANK = 512
U_FLOOR = 1e-10
LN_EPS = 1e-5
UNIT = 2.0 ** -53
STEEP = -3.0e38
LOWEST = -3.0e38
SLOPE = 0.2
TABLES = "natural_log_exp_and_others"


class Steps:

    def __init__(self, sem, names):
        self.sem, self.names = sem, list(names)
        assert len(set(self.names)) == len(self.names)

    def at(self, n, name):
        return n * len(self.names) + self.names.index(name) + 1

    def all(self, rounds):
        return rounds * len(self.names)


def ln_vector_steps(tag):
    return [f"{s}_{tag}" for s in ("sum", "mean", "center", "power", "var", "seed2", "seed2var", "fix", "rstd")]


def ln_scalar_steps(tag):
    return [f"{s}_{tag}" for s in ("square", "log", "seed")]


def per_tile(stat, width):
    return stat.unsqueeze(2).broadcast_to([stat.shape[0], stat.shape[1], width])


def per_column(row, tiles):
    return row.unsqueeze(1).broadcast_to([row.shape[0], tiles, row.shape[1]])


def build(nc, x, adj, u, W1, b1, W2, b2, Wg, bg, Wn, bn, g_in, b_in, g_out, b_out, W, b, a_s, a_r, out):
    N, D = x.shape
    NT = N // P
    GT = 4
    NG = NT // GT
    CW = 1024
    NC = N // CW
    SLOTS0 = 3
    UB = 2
    UC = CW // P // UB
    UG = NC * UC
    PW = GT * P
    PTL = CW // P
    NP = NT // PTL
    HALF = N // 2
    SLOTS1 = 4
    VB = 6
    VU = NT // VB
    NQ = NT // 2
    NI = NT // SLOTS1
    CONSTS = 17
    assert D == P and NC % SLOTS0 == 0 and UG % 2 == 0 and NP == NC and VU == 8 and NC * CW == N

    with ExitStack() as ctx:
        def sb(name, shape, dt=F32):
            return ctx.enter_context(nc.sbuf_tensor(name, shape, dt))

        def sem(name):
            return ctx.enter_context(nc.semaphore(name))

        feats = sb("feats", [P, NT, D])
        r_row = sb("r_row", [P, N])
        s_col = sb("s_col", [P, NT])
        gate = sb("gate", [P, NT])
        ident = sb("ident", [P, P])
        wcat = sb("wcat", [P, 2, 2 * P])
        wn_sb = sb("wn_sb", [P, 2])
        wT = sb("wT", [P, P])
        wraw = sb("wraw", [P, P])
        bcat = sb("bcat", [P, 2 * P])
        rows = sb("rows", [P, 6, P])
        ROW = {n: rows[:, i, :] for i, n in enumerate(("b2", "g_in", "b_in", "g_out", "b_out", "b"))}
        vecs = sb("vecs", [P, 3])
        a_wide = sb("a_wide", [P, P + 1])
        b_wide = sb("b_wide", [P, P])
        wa = sb("wa", [P, P + 1])
        ba = sb("ba", [P, 2])
        bn_row = sb("bn_row", [P, 2])
        noise = sb("noise", [P, NT, 2])
        lstat = sb("lstat", [P, 10, PTL])
        zbuf = sb("zbuf", [P, 2, PTL, 2])
        zstat = sb("zstat", [P, 6, PTL])
        eps = sb("eps", [P, 2])
        ones = sb("ones", [P, 1])

        def tiles(a, n=GT):
            return a.rearrange("p (t d) -> p t d", t=n)

        with ExitStack() as l0:
            def sb0(name, shape, dt=F32):
                return l0.enter_context(nc.sbuf_tensor(name, shape, dt))

            ring_mem = sb0("ring_mem", [P, SLOTS0 * GT * CW])
            ring = [ring_mem[:, s * GT * CW:(s + 1) * GT * CW].rearrange("p (t c) -> p t c", t=GT)
                    for s in range(SLOTS0)]
            gated_hi = sb0("gated_hi", [P, NT, D], F32R)
            gated_lo = sb0("gated_lo", [P, NT, D], F32R)
            turned_hi = [sb0(f"turned_hi{i}", [P, UB * PW], F32R) for i in range(2)]
            turned_lo = [sb0(f"turned_lo{i}", [P, UB * PW], F32R) for i in range(2)]
            PX = PTL * D
            scratch = sb0("scratch", [P, 7 * PX])
        x8 = [scratch[:, i * PX:(i + 1) * PX] for i in range(2)]
        xn8, sq8 = (scratch[:, i * PX:(i + 1) * PX] for i in (2, 3))
        xnT8 = sq8
        carry8 = tiles(scratch[:, 4 * PX:7 * PX], PTL)
        carry_in = tiles(scratch[:, 0:GT * 3 * P])
        e0 = GT * 3 * P
        x_in, rawT, fg, v2, dlt, y, sq, h1, h1T = (scratch[:, e0 + i * PW:e0 + (i + 1) * PW] for i in range(9))
        assert e0 + 9 * PW <= 7 * PX
        stage = sb("stage", [P, SLOTS1 * N])
        slot = [stage[:, s * N:(s + 1) * N] for s in range(SLOTS1)]
        probT = [sb(f"probT{i}", [P, VB * 2 * P]) for i in range(2)]
        mask = [sb(f"mask{i}", [P, HALF], U8) for i in range(2)]
        maxes = sb("maxes", [P, 2])
        top = sb("top", [P, 1])
        negmax = sb("negmax", [P, SLOTS1])
        sums = sb("sums", [P, SLOTS1, 2])
        rinv = sb("rinv", [P, 2])
        oT = sb("oT", [P, 2 * P])
        x1_in = sb("x1_in", [P, 2, P])
        fin = sb("fin", [P, 2, P])

        psum = ctx.enter_context(nc.psum_tensor("psum", [P, 8 * BANK], F32))

        def bank(i, n=1):
            return psum[:, i * BANK:(i + n) * BANK]

        turning0 = [bank(0, 2), bank(2, 2)]
        acc0 = bank(4)
        ep = [bank(5), bank(6), bank(7)]
        turning1 = [bank(0, 3), bank(3, 3)]
        acc1 = [bank(6)[:, 0:2 * P], bank(7)[:, 0:2 * P]]
        final = [bank(6)[:, 2 * P:4 * P], bank(7)[:, 2 * P:4 * P]]

        carry = nc.dram_tensor("carry", (N, 3 * P), F32, kind="Internal").ap()
        x_mid = nc.dram_tensor("x_mid", (N, D), F32, kind="Internal").ap()

        def by_tile(a):
            return a.rearrange("(t p) d -> p t d", p=P)

        consts_in = sem("consts_in")
        noise_in = sem("noise_in")
        x_loaded = [sem("x_loaded0"), sem("x_loaded1")]
        ident_ready = sem("ident_ready")
        noise_vec = Steps(sem("noise_vec"), ["eps_log", "eps_ln", "one", "clipped", "bias"])
        noise_act = Steps(sem("noise_act"), ["log", "loglog"])
        wT_turned = sem("wT_turned")
        attend = Steps(sem("attend"), ["a_s", "a_r", "b", "wT", "wa", "ba"])
        piece_vec = Steps(sem("piece_vec"), [
            *ln_vector_steps("x"), "h", *ln_vector_steps("h"), "normed", "scaled", "xn",
            "z", "zmax", "zsub", "esum", "erec", "p1", "hard", "y", "gate", "gated", "hi", "lo", "mix0", "mix1", "mix2", "mix3"])
        piece_act = Steps(sem("piece_act"), [*ln_scalar_steps("x"), *ln_scalar_steps("h"), "xnT0", "xnT1", "exp"])
        piece_pe = Steps(sem("piece_pe"), ["turn0", "turn1", "logits", "mix0", "mix1", "mix2", "mix3"])
        carry_stored = sem("carry_stored")
        chunk_full = [sem(f"chunk_full{s}") for s in range(SLOTS0)]
        blocks_turned = sem("blocks_turned")
        lo_ready = [sem("lo_ready0"), sem("lo_ready1")]
        hi_ready = [sem("hi_ready0"), sem("hi_ready1")]
        unit_summed = sem("unit_summed")
        acc_copied = sem("acc_copied")
        epi_vec = Steps(sem("epi_vec"), [
            *(f"gpre{t}" for t in range(GT)), *(f"view2_{t}" for t in range(GT)),
            "gap", "one_plus", *(f"sigmoid{t}" for t in range(GT)), "mixed", "fused", "resid",
            *ln_vector_steps("out"), "normed", "scaled", "shifted", "x_mid",
            *ln_vector_steps("next"), "h1", "H", "s"])
        epi_act = Steps(sem("epi_act"), ["exp", *ln_scalar_steps("out"), *ln_scalar_steps("next"), "h1T", "r_row"])
        epi_pe = Steps(sem("epi_pe"), ["mix01", "mix23", "turn", "H", "s", "r_row"])
        carry_loaded = sem("carry_loaded")
        x_mid_stored = sem("x_mid_stored")
        half_full = [[sem(f"half_full{s}_{c}") for c in range(2)] for s in range(SLOTS1)]
        leaky_ready = sem("leaky_ready")
        mask_ready = sem("mask_ready")
        sums_copied = sem("sums_copied")
        product_ready = sem("product_ready")
        half_max = sem("half_max")
        top_ready, max_ready = sem("top_ready"), sem("max_ready")
        exp_done = sem("exp_done")
        probs_turned = sem("probs_turned")
        probT_ready = [sem("probT_ready0"), sem("probT_ready1")]
        probs_summed = sem("probs_summed")
        fin_vec = Steps(sem("fin_vec"), ["total", "rinv", "scaled", "out"])
        fin_turned = sem("fin_turned")
        xm_loaded = sem("xm_loaded")
        out_stored = sem("out_stored")

        waits_met = sem("waits_met")

        def met(engine):
            engine.sem_inc(waits_met, 1)

        def at_slot(i, s):
            return i + s // SLOTS1, s % SLOTS1

        block = ctx.enter_context(nc.Block())

        @block.sync
        def _(sp):
            def load_piece(n):
                if n >= 2:
                    sp.wait_ge(piece_vec.sem, piece_vec.at(n - 2, "center_x"))
                sp.dma_start(tiles(x8[n % 2], PTL), by_tile(x)[:, n * PTL:(n + 1) * PTL, :]).then_inc(x_loaded[n % 2], 16)

            def store_carry(n):
                sp.wait_ge(piece_vec.sem, piece_vec.at(n, "mix3"))
                sp.dma_start(by_tile(carry)[:, n * PTL:(n + 1) * PTL, :], carry8).then_inc(carry_stored, 16)

            adj_groups = adj.rearrange("(g t p) c -> g p t c", t=GT, p=P)

            def load_chunk(g, c, first):
                s = c % SLOTS0
                if not (first and c < SLOTS0):
                    sp.wait_ge(blocks_turned, g * UG + (c - SLOTS0 + 1) * UC)
                sp.dma_start(ring[s], adj_groups[g, :, :, c * CW:(c + 1) * CW]).then_inc(chunk_full[s], 16)

            def load_carry(g):
                sp.wait_ge(x_mid_stored, 16 * g)
                fetch_carry(g)

            def fetch_carry(g):
                sp.dma_start(carry_in, by_tile(carry)[:, bass.ts(g, GT), :]).then_inc(carry_loaded, 16)
                sp.dma_start(tiles(x_in), by_tile(x)[:, bass.ts(g, GT), :]).then_inc(carry_loaded, 16)

            def store_x_mid(g):
                sp.wait_ge(epi_vec.sem, epi_vec.at(g, "x_mid"))
                sp.dma_start(by_tile(x_mid)[:, bass.ts(g, GT), :], tiles(y)).then_inc(x_mid_stored, 16)

            load_piece(0)
            for src, dst in ((u.rearrange("(t p) k -> p t k", p=P), noise[:]),
                             (bn.partition_broadcast(P), bn_row[:])):
                sp.dma_start(dst, src).then_inc(noise_in, 16)
            for src, dst in ((Wg[0:P, :], wcat[:, 0, 0:P]), (W1, wcat[:, 0, P:2 * P]),
                             (Wg[P:2 * P, :], wcat[:, 1, 0:P]), (W2, wcat[:, 1, P:2 * P]),
                             (Wn, wn_sb[:]), (W, wraw[:]),
                             (bg.partition_broadcast(P), bcat[:, 0:P]), (b1.partition_broadcast(P), bcat[:, P:2 * P]),
                             (b2.partition_broadcast(P), ROW["b2"]), (g_in.partition_broadcast(P), ROW["g_in"]),
                             (b_in.partition_broadcast(P), ROW["b_in"]), (g_out.partition_broadcast(P), ROW["g_out"]),
                             (b_out.partition_broadcast(P), ROW["b_out"]), (b.partition_broadcast(P), ROW["b"]),
                             (a_s, vecs[:, 0:1]), (a_r, vecs[:, 1:2]),
                             (b.rearrange("(d k) -> d k", k=1), vecs[:, 2:3])):
                sp.dma_start(dst, src).then_inc(consts_in, 16)
            load_piece(1)
            for c in range(SLOTS0):
                load_chunk(0, c, True)
            for n in range(2, NP):
                load_piece(n)
                store_carry(n - 2)
                if n - 2 + SLOTS0 < NC:
                    load_chunk(0, n - 2 + SLOTS0, True)
            store_carry(NP - 2)
            store_carry(NP - 1)
            sp.wait_ge(carry_stored, 16 * NP)
            fetch_carry(0)
            with sp.Fori(1, NG) as g:
                for c in range(NC):
                    load_chunk(g, c, False)
                store_x_mid(g - 1)
                load_carry(g)
            store_x_mid(NG - 1)

            adj_tiles = adj.rearrange("(t p) c -> t p c", p=P)

            def load_half(k, s, c):
                sp.dma_start(slot[s][:, c * HALF:(c + 1) * HALF],
                             adj_tiles[k, :, c * HALF:(c + 1) * HALF]).then_inc(half_full[s][c], 16)

            for s in range(SLOTS1):
                if s == 0:
                    sp.wait_ge(blocks_turned, NG * UG)
                if s == 2:
                    sp.wait_ge(unit_summed, NG * UG)
                for c in range(2):
                    load_half(s, s, c)
            with sp.Fori(1, NI) as i:
                for q in range(2):
                    for c in range(2):
                        sp.wait_ge(probs_turned, (2 * i + q - 2) * VU + (c + 1) * (VU // 2))
                        for s in (2 * q, 2 * q + 1):
                            load_half(SLOTS1 * i + s, s, c)

        @block.gpsimd
        def _(pool):
            pool.memset(ident[:], 0.0).then_inc(ident_ready, 1)
            pool.wait_ge(ident_ready, 1)
            pool.affine_select(out=ident[:], in_=ident[:], compare_op=ALU.not_equal, fill=1.0, base=0,
                               pattern=[[-1, P]], channel_multiplier=1).then_inc(ident_ready, 1)
            pool.wait_ge(x_mid_stored, 16 * NG)

            def finish(q):
                pool.dma_start(x1_in[:], by_tile(x_mid)[:, bass.ts(q, 2), :]).then_inc(xm_loaded, 16)
                pool.wait_ge(fin_vec.sem, fin_vec.at(q, "out"))
                met(pool)
                pool.dma_start(by_tile(out)[:, bass.ts(q, 2), :], fin[:]).then_inc(out_stored, 16)
                pool.wait_ge(out_stored, 16 * (q + 1))

            with pool.Fori(0, NQ) as q:
                finish(q)

        @block.scalar
        def _(act):
            def ln_square(steps, vec, n, tag, src, dst):
                act.wait_ge(vec.sem, vec.at(n, f"center_{tag}"))
                act.activation(dst, src, ACT.Square).then_inc(steps.sem, 1)

            def ln_seed(steps, vec, n, tag, stat):
                act.wait_ge(vec.sem, vec.at(n, f"power_{tag}"))
                act.activation(stat[3], stat[2], ACT.Ln, scale=1.0 / D, bias=eps[:, 0:1]).then_inc(steps.sem, 1)
                act.wait_ge(steps.sem, steps.at(n, f"log_{tag}"))
                act.activation(stat[4], stat[3], ACT.Exp, scale=-0.5).then_inc(steps.sem, 1)

            act.preload_act_table_set(TABLES)
            act.wait_ge(noise_vec.sem, noise_vec.at(0, "clipped"))
            act.activation(noise[:], noise[:], ACT.Ln).then_inc(noise_act.sem, 1)
            act.wait_ge(noise_act.sem, noise_act.at(0, "log"))
            act.activation(noise[:], noise[:], ACT.Ln, scale=-1.0, bias=eps[:, 1:2]).then_inc(noise_act.sem, 1)

            def piece_steps(n):
                st = [lstat[:, i, :] for i in range(10)]

                def norms_x():
                    ln_square(piece_act, piece_vec, n, "x", xn8, sq8)
                    ln_seed(piece_act, piece_vec, n, "x", st)

                def norms_h():
                    ln_square(piece_act, piece_vec, n, "h", xn8, sq8)
                    ln_seed(piece_act, piece_vec, n, "h", st)

                def copies():
                    for i in range(2):
                        act.wait_ge(piece_pe.sem, piece_pe.at(n, f"turn{i}"))
                        act.activation(xnT8[:, i * BANK:(i + 1) * BANK], ep[i], ACT.Copy).then_inc(piece_act.sem, 1)

                def exps():
                    act.wait_ge(piece_vec.sem, piece_vec.at(n, "zsub"))
                    act.activation(zbuf[:, 1], zbuf[:, 0], ACT.Exp).then_inc(piece_act.sem, 1)
                return [norms_x, norms_h, copies, exps]

            def evacuate(g, v, first):
                n = g * UG + v
                act.wait_ge(blocks_turned, n + 1)
                if not (first and v < 2):
                    act.wait_ge(unit_summed, n - 1)
                act.activation(turned_hi[v % 2][:], turning0[v % 2], ACT.Copy).then_inc(hi_ready[v % 2], 1)

            def copy_acc(g):
                act.wait_ge(unit_summed, (g + 1) * UG)
                act.activation(rawT, acc0, ACT.Copy).then_inc(acc_copied, 1)

            estat = [lstat[:, i, 0:GT] for i in range(10)]

            def epi_exp(g):
                act.wait_ge(epi_vec.sem, epi_vec.at(g, f"view2_{GT - 1}"))
                act.activation(fg, fg, ACT.Exp, scale=-1.0).then_inc(epi_act.sem, 1)

            def epi_turn(g):
                act.wait_ge(epi_pe.sem, epi_pe.at(g, "turn"))
                act.activation(h1T, ep[2], ACT.Copy).then_inc(epi_act.sem, 1)

            def epi_r(g):
                act.wait_ge(epi_pe.sem, epi_pe.at(g, "r_row"))
                act.activation(r_row[:, bass.ts(g, PW)], ep[1], ACT.Identity, bias=ba[:, 0:1]).then_inc(epi_act.sem, 1)

            def epilogue(g):
                return {3: [lambda: epi_exp(g)],
                        12: [lambda: ln_square(epi_act, epi_vec, g, "out", dlt, sq)],
                        13: [lambda: ln_seed(epi_act, epi_vec, g, "out", estat)],
                        17: [lambda: ln_square(epi_act, epi_vec, g, "next", dlt, sq)],
                        18: [lambda: ln_seed(epi_act, epi_vec, g, "next", estat)],
                        20: [lambda: epi_turn(g)],
                        23: [lambda: epi_r(g)]}

            for f in piece_steps(0):
                f()
            for c in range(NC):
                norms_x, norms_h, copies, exps_z = piece_steps(min(c + 1, NP - 1))
                between = [[norms_x], [norms_h], [copies, exps_z], []] if c + 1 < NP else [[]] * UC
                for w in range(UC):
                    evacuate(0, c * UC + w, True)
                    for f in between[w]:
                        f()
            with act.Fori(1, NG) as g:
                todo = epilogue(g - 1)
                for v in range(UG):
                    evacuate(g, v, False)
                    if v == 0:
                        copy_acc(g - 1)
                    for f in todo.get(v, []):
                        f()
            copy_acc(NG - 1)
            for fs in epilogue(NG - 1).values():
                for f in fs:
                    f()

            def masks(i, s, c, first=False):
                i, s = at_slot(i, s)
                act.wait_ge(half_full[s][c], 16 * (i + 1))
                if not first:
                    act.wait_ge(half_max, 2 * (SLOTS1 * i + s) + c - 1)
                act.activation(mask[c][:], slot[s][:, c * HALF:(c + 1) * HALF], ACT.Relu,
                               scale=STEEP, bias=ones[:]).then_inc(mask_ready, 1)

            def exps(i, s, c, first):
                i, s = at_slot(i, s)
                act.wait_ge(max_ready, SLOTS1 * i + s + 1)
                if c == 0 and not first:
                    act.wait_ge(fin_vec.sem, fin_vec.at(2 * i + s // 2 - 2, "total"))
                half = slot[s][:, c * HALF:(c + 1) * HALF]
                act.activation(half, half, ACT.Exp, bias=negmax[:, s:s + 1], scale=1.0 / UNIT,
                               accum_out=sums[:, s, c:c + 1]).then_inc(exp_done, 1)

            def evacuate1(i, s, v, first):
                i, s = at_slot(i, s)
                n = (2 * i + s // 2) * VU + v
                act.wait_ge(probs_turned, n + 1)
                if not (first and v < 2):
                    act.wait_ge(probs_summed, n - 1)
                act.activation(probT[v % 2][:], turning1[v % 2], ACT.Copy).then_inc(probT_ready[v % 2], 1)

            def copy_sums(q, qs):
                act.wait_ge(probs_summed, VU * (q + 1))
                if not (isinstance(q, int) and q == 0):
                    act.wait_ge(fin_turned, q)
                act.activation(oT[:], acc1[qs], ACT.Copy).then_inc(sums_copied, 1)

            def step(i, s, start=False, fresh=False, last=False, here=True):
                quarter = VU // 2 * (s % 2)
                for c in range(2):
                    if not (start and s == 0):
                        exps(i, s - 1, c, start or fresh)
                    if c == 0 and here:
                        masks(i, s, 1, start and s == 0)
                    if c == 1 and not last:
                        masks(i, s + 1, 0, False)
                    if not (start and s < 2):
                        for v in (quarter + 2 * c, quarter + 2 * c + 1):
                            evacuate1(i, s - 2, v, start and s == 2)
                            if v == 1 and not start:
                                j, t = at_slot(i, s - 4)
                                copy_sums(2 * j + t // 2, t // 2)

            act.wait_ge(unit_summed, NG * UG)
            act.wait_ge(epi_vec.sem, epi_vec.all(NG))
            act.wait_ge(epi_pe.sem, epi_pe.all(NG))
            masks(0, 0, 0, True)
            for s in range(SLOTS1):
                step(0, s, start=True)
            step(1, 0, fresh=True)
            with act.Fori(1, NI - 1) as i:
                for s in range(1, SLOTS1 + 1):
                    step(*at_slot(i, s))
            for s in range(1, SLOTS1 + 1):
                step(NI - 1, s, last=s >= SLOTS1 - 1, here=s < SLOTS1)
            for v in range(VU // 2, VU):
                evacuate1(NI - 1, 2, v, False)
            copy_sums(NQ - 1, 1)

        @block.tensor
        def _(pe):
            pe.wait_ge(ident_ready, 2)
            pe.wait_ge(consts_in, 16 * CONSTS)
            pe.transpose(ep[2][:, P:2 * P], wraw[:], ident[:])
            pe.wait_ge(attend.sem, attend.at(0, "b"))
            pe.matmul(ep[1][:, 0:P + 1], wraw[:], a_wide[:], start=True, stop=True)
            pe.matmul(ep[1][:, P + 1:P + 3], b_wide[:], a_wide[:, P - 1:P + 1], start=True,
                      stop=True).then_inc(wT_turned, 1)

            def piece_turn(n):
                pe.wait_ge(piece_vec.sem, piece_vec.at(n, "xn"))
                if n == 0:
                    pe.wait_ge(attend.sem, attend.all(1))
                for i in range(2):
                    if n >= 1:
                        pe.wait_ge(piece_vec.sem, piece_vec.at(n - 1, f"mix{2 + i}"))
                    for t in range(4):
                        mm = pe.transpose(ep[i][:, t * P:(t + 1) * P], tiles(xn8, PTL)[:, 4 * i + t, :], ident[:])
                    mm.then_inc(piece_pe.sem, 1)

            def piece_logits(n):
                pe.wait_ge(piece_act.sem, piece_act.at(n, "xnT1"))
                for t in range(PTL):
                    mm = pe.matmul(ep[2][:, 2 * t:2 * t + 2], xnT8[:, t * P:(t + 1) * P], wn_sb[:], start=True, stop=True)
                mm.then_inc(piece_pe.sem, 1)

            def piece_mix(n):
                for i in range(4):
                    if i >= 2:
                        pe.wait_ge(piece_vec.sem, piece_vec.at(n, f"mix{i - 2}"))
                    for t in range(2):
                        mm = pe.matmul(ep[i % 2][:, t * 2 * P:(t + 1) * 2 * P], xnT8[:, (2 * i + t) * P:(2 * i + t + 1) * P],
                                       wcat[:, 0, :], start=True, stop=True)
                    mm.then_inc(piece_pe.sem, 1)

            def turn(g, v, first):
                n = g * UG + v
                c, w = v // UC, v % UC
                s = c % SLOTS0
                if w == 0:
                    pe.wait_ge(chunk_full[s], 16 * (g * (NC // SLOTS0) + c // SLOTS0 + 1))
                if not (first and v < 2):
                    pe.wait_ge(lo_ready[v % 2], g * (UG // 2) + v // 2)
                for j in range(UB):
                    for t in range(GT):
                        mm = pe.transpose(turning0[v % 2][:, j * PW + t * P:j * PW + (t + 1) * P],
                                          ring[s][:, t, (w * UB + j) * P:(w * UB + j + 1) * P], ident[:])
                mm.then_inc(blocks_turned, 1)

            def gather(g, v, first):
                if first and v % UC == 0:
                    pe.wait_ge(piece_vec.sem, piece_vec.at(v // UC, "lo"))
                if v == 0 and not first:
                    pe.wait_ge(acc_copied, g)
                pe.wait_ge(hi_ready[v % 2], g * (UG // 2) + v // 2 + 1)
                for j in range(UB):
                    blk = v * UB + j
                    cols = slice(j * PW, (j + 1) * PW)
                    pe.matmul(acc0, gated_hi[:, blk, :], turned_hi[v % 2][:, cols], start=blk == 0, stop=False)
                    pe.matmul(acc0, gated_lo[:, blk, :], turned_hi[v % 2][:, cols], start=False, stop=False)
                    if j == 0:
                        pe.wait_ge(lo_ready[v % 2], g * (UG // 2) + v // 2 + 1)
                    mm = pe.matmul(acc0, gated_hi[:, blk, :], turned_lo[v % 2][:, cols], start=False,
                                   stop=blk == NT - 1)
                mm.then_inc(unit_summed, 1)

            def epi_mix(g, i):
                if i == 0:
                    pe.wait_ge(acc_copied, g + 1)
                    pe.wait_ge(piece_vec.sem, piece_vec.all(NP))
                for t in range(2):
                    mm = pe.matmul(ep[i][:, t * 2 * P:(t + 1) * 2 * P], rawT[:, (2 * i + t) * P:(2 * i + t + 1) * P],
                                   wcat[:, 1, :], start=True, stop=True)
                mm.then_inc(epi_pe.sem, 1)

            def epi_turn(g):
                pe.wait_ge(epi_vec.sem, epi_vec.at(g, "h1"))
                for t in range(GT):
                    mm = pe.transpose(ep[2][:, t * P:(t + 1) * P], h1[:, t * P:(t + 1) * P], ident[:])
                mm.then_inc(epi_pe.sem, 1)

            def epi_h(g):
                pe.wait_ge(epi_act.sem, epi_act.at(g, "h1T"))
                for t in range(GT):
                    mm = pe.matmul(ep[0][:, t * P:(t + 1) * P], h1T[:, t * P:(t + 1) * P], wT[:], start=True, stop=True)
                mm.then_inc(epi_pe.sem, 1)
                for t in range(GT):
                    mm = pe.matmul(ep[2][:, t:t + 1], h1T[:, t * P:(t + 1) * P], wa[:, P:P + 1], start=True, stop=True)
                mm.then_inc(epi_pe.sem, 1)

            def epi_r(g):
                pe.matmul(ep[1], wa[:, 0:P], h1T, start=True, stop=True).then_inc(epi_pe.sem, 1)

            def epilogue(g):
                return {0: [lambda: epi_mix(g, 0)], 1: [lambda: epi_mix(g, 1)], 18: [lambda: epi_turn(g)],
                        20: [lambda: epi_h(g)], 21: [lambda: epi_r(g)]}

            piece_turn(0)
            piece_logits(0)
            piece_mix(0)
            for v in range(UG):
                turn(0, v, True)
                if v >= 1:
                    gather(0, v - 1, True)
                if v // UC + 1 < NP:
                    for f in {2: (piece_turn, piece_logits), 3: (piece_mix,)}.get(v % UC, ()):
                        f(v // UC + 1)
            with pe.Fori(1, NG) as g:
                todo = epilogue(g - 1)
                for v in range(UG):
                    turn(g, v, False)
                    if v == 0:
                        gather(g - 1, UG - 1, False)
                    else:
                        gather(g, v - 1, False)
                    for f in todo.get(v - 1, []):
                        f()
            gather(NG - 1, UG - 1, False)
            for fs in epilogue(NG - 1).values():
                for f in fs:
                    f()

            def turn1(q, qs, v, first):
                c = v // (VU // 2)
                if v % (VU // 2) == 0:
                    pe.wait_ge(exp_done, 2 * (2 * q + 1) + c + 1)
                if not (first and v < 2):
                    pe.wait_ge(probT_ready[v % 2], q * (VU // 2) + v // 2)
                for j in range(VB):
                    for t in range(2):
                        mm = pe.transpose(turning1[v % 2][:, (2 * j + t) * P:(2 * j + t + 1) * P],
                                          slot[2 * qs + t][:, (v * VB + j) * P:(v * VB + j + 1) * P], ident[:])
                mm.then_inc(probs_turned, 1)

            def gather1(q, qs, v):
                pe.wait_ge(probT_ready[v % 2], q * (VU // 2) + v // 2 + 1)
                for j in range(VB):
                    blk = v * VB + j
                    mm = pe.matmul(acc1[qs], feats[:, blk, :], probT[v % 2][:, j * 2 * P:(j + 1) * 2 * P],
                                   start=blk == 0, stop=blk == NT - 1)
                mm.then_inc(probs_summed, 1)

            def turn_sums(q, qs):
                pe.wait_ge(sums_copied, q + 1)
                for t in range(2):
                    mm = pe.transpose(final[qs][:, t * P:(t + 1) * P], oT[:, t * P:(t + 1) * P], ident[:])
                mm.then_inc(fin_turned, 1)

            def pair(q, qs, first):
                for v in range(VU):
                    turn1(q, qs, v, first)
                    if v == 0 and not first:
                        gather1(q - 1, 1 - qs, VU - 1)
                    if v >= 1:
                        gather1(q, qs, v - 1)
                    if v == 2 and not first:
                        turn_sums(q - 1, 1 - qs)

            pe.wait_ge(epi_vec.sem, epi_vec.all(NG))
            pe.wait_ge(epi_act.sem, epi_act.all(NG))
            pair(0, 0, True)
            pair(1, 1, False)
            with pe.Fori(1, NI) as i:
                pair(2 * i, 0, False)
                pair(2 * i + 1, 1, False)
            gather1(NQ - 1, 1, VU - 1)
            turn_sums(NQ - 1, 1)

        @block.vector
        def _(vec):
            def ln_center(steps, n, tag, src, center, stat, tl):
                ssum, nmean = stat[:2]

                def done(name):
                    vec.wait_ge(steps.sem, steps.at(n, name))

                vec.tensor_reduce(ssum, src, AX.X, ALU.add).then_inc(steps.sem, 1)
                done(f"sum_{tag}")
                vec.tensor_scalar(nmean, ssum, -1.0 / D, None, ALU.mult).then_inc(steps.sem, 1)
                done(f"mean_{tag}")
                vec.tensor_tensor(tiles(center, tl), src, per_tile(nmean, D), ALU.add).then_inc(steps.sem, 1)

            def ln_power(steps, acts, n, tag, sq_, stat, tl):
                _, _, power, _, _, var, _, _, _, _ = stat
                vec.wait_ge(acts.sem, acts.at(n, f"square_{tag}"))
                vec.tensor_reduce(power, tiles(sq_, tl), AX.X, ALU.add).then_inc(steps.sem, 1)
                vec.wait_ge(steps.sem, steps.at(n, f"power_{tag}"))
                vec.tensor_scalar(var, power, 1.0 / D, LN_EPS, ALU.mult, ALU.add).then_inc(steps.sem, 1)

            def ln_rstd(steps, acts, n, tag, stat):
                _, _, _, _, seed, var, s2, s2v, fix, rstd = stat

                def done(name):
                    vec.wait_ge(steps.sem, steps.at(n, name))

                vec.wait_ge(acts.sem, acts.at(n, f"seed_{tag}"))
                vec.tensor_tensor(s2, seed, seed, ALU.mult).then_inc(steps.sem, 1)
                done(f"seed2_{tag}")
                vec.tensor_tensor(s2v, s2, var, ALU.mult).then_inc(steps.sem, 1)
                done(f"seed2var_{tag}")
                vec.tensor_scalar(fix, s2v, -0.5, 1.5, ALU.mult, ALU.add).then_inc(steps.sem, 1)
                done(f"fix_{tag}")
                vec.tensor_tensor(rstd, seed, fix, ALU.mult).then_inc(steps.sem, 1)
                done(f"rstd_{tag}")

            vec.wait_ge(consts_in, 16 * CONSTS)
            vec.tensor_scalar(a_wide[:, P:P + 1], vecs[:, 0:1], UNIT, None, ALU.mult).then_inc(attend.sem, 1)
            vec.tensor_scalar(a_wide[:, 0:P], vecs[:, 1:2].broadcast_to([P, P]), UNIT, None,
                              ALU.mult).then_inc(attend.sem, 1)
            vec.tensor_copy(b_wide[:], vecs[:, 2:3].broadcast_to([P, P])).then_inc(attend.sem, 1)
            vec.wait_ge(wT_turned, 1)
            vec.tensor_copy(wT[:], ep[2][:, P:2 * P]).then_inc(attend.sem, 1)
            vec.tensor_copy(wa[:], ep[1][:, 0:P + 1]).then_inc(attend.sem, 1)
            vec.tensor_copy(ba[:], ep[1][:, P + 1:P + 3]).then_inc(attend.sem, 1)
            vec.memset(eps[:, 0:1], LN_EPS).then_inc(noise_vec.sem, 1)
            vec.memset(eps[:, 1:2], U_FLOOR).then_inc(noise_vec.sem, 1)
            vec.memset(ones[:], 1.0).then_inc(noise_vec.sem, 1)
            vec.wait_ge(noise_in, 32)
            vec.tensor_scalar(noise[:], noise[:], U_FLOOR, 1.0, ALU.max, ALU.min).then_inc(noise_vec.sem, 1)
            vec.wait_ge(noise_act.sem, noise_act.at(0, "loglog"))
            vec.tensor_tensor(noise[:], per_column(bn_row[:], NT), noise[:], ALU.subtract).then_inc(noise_vec.sem, 1)

            ps = piece_vec
            pstat = [lstat[:, i, :] for i in range(10)]

            def piece_done(n):
                def done(name):
                    vec.wait_ge(ps.sem, ps.at(n, name))
                return done

            def piece_h(n):
                st = pstat
                vec.wait_ge(x_loaded[n % 2], 16 * (n // 2 + 1))
                ln_center(ps, n, "x", tiles(x8[n % 2], PTL), xn8, st, PTL)
                ln_power(ps, piece_act, n, "x", sq8, st, PTL)
                ln_rstd(ps, piece_act, n, "x", st)
                if n >= 1:
                    vec.wait_ge(carry_stored, 16 * n)
                h8 = carry8[:, :, 2 * P:3 * P]
                vec.scalar_tensor_tensor(h8, tiles(xn8, PTL), 0.0, per_tile(st[9], D), ALU.max, ALU.mult).then_inc(ps.sem, 1)

            def piece_xn(n):
                st, done = pstat, piece_done(n)
                h8 = carry8[:, :, 2 * P:3 * P]
                done("h")
                ln_center(ps, n, "h", h8, xn8, st, PTL)
                ln_power(ps, piece_act, n, "h", sq8, st, PTL)
                ln_rstd(ps, piece_act, n, "h", st)
                vec.tensor_tensor(tiles(xn8, PTL), tiles(xn8, PTL), per_tile(st[9], D), ALU.mult).then_inc(ps.sem, 1)
                done("normed")
                vec.tensor_tensor(tiles(xn8, PTL), tiles(xn8, PTL), per_column(ROW["g_in"], PTL), ALU.mult).then_inc(ps.sem, 1)
                done("scaled")
                vec.tensor_tensor(tiles(xn8, PTL), tiles(xn8, PTL), per_column(ROW["b_in"], PTL), ALU.add).then_inc(ps.sem, 1)
                if n == 0:
                    vec.wait_ge(noise_vec.sem, noise_vec.at(0, "bias"))

            def piece_gate(n):
                done = piece_done(n)
                z, e = zbuf[:, 0], zbuf[:, 1]
                zmax, esum, erec, p1, hard, ysum = (zstat[:, i, :] for i in range(6))
                vec.wait_ge(piece_pe.sem, piece_pe.at(n, "logits"))
                vec.tensor_tensor(z, ep[2][:, 0:2 * PTL].rearrange("p (t k) -> p t k", k=2),
                                  noise[:, n * PTL:(n + 1) * PTL, :], ALU.add).then_inc(ps.sem, 1)
                done("z")
                vec.tensor_tensor(zmax, z[:, :, 0], z[:, :, 1], ALU.max).then_inc(ps.sem, 1)
                done("zmax")
                vec.tensor_tensor(z, z, per_tile(zmax, 2), ALU.subtract).then_inc(ps.sem, 1)
                vec.wait_ge(piece_act.sem, piece_act.at(n, "exp"))
                vec.tensor_tensor(esum, e[:, :, 0], e[:, :, 1], ALU.add).then_inc(ps.sem, 1)
                done("esum")
                vec.reciprocal(erec, esum).then_inc(ps.sem, 1)
                done("erec")
                vec.tensor_tensor(p1, e[:, :, 1], erec, ALU.mult).then_inc(ps.sem, 1)
                vec.tensor_tensor(hard, z[:, :, 1], z[:, :, 0], ALU.is_gt).then_inc(ps.sem, 1)
                done("hard")
                vec.tensor_tensor(ysum, hard, p1, ALU.add).then_inc(ps.sem, 1)
                done("y")
                vec.tensor_tensor(gate[:, n * PTL:(n + 1) * PTL], ysum, p1, ALU.subtract).then_inc(ps.sem, 1)
                done("gate")
                here = slice(n * PTL, (n + 1) * PTL)
                vec.wait_ge(piece_pe.sem, piece_pe.at(n, "turn1"))
                vec.tensor_tensor(tiles(xn8, PTL), tiles(xn8, PTL), per_tile(gate[:, here], D), ALU.mult).then_inc(ps.sem, 1)
                done("gated")
                vec.tensor_copy(gated_hi[:, here, :], tiles(xn8, PTL)).then_inc(ps.sem, 1)
                done("hi")
                vec.tensor_tensor(gated_lo[:, here, :], tiles(xn8, PTL), gated_hi[:, here, :].bitcast(F32),
                                  ALU.subtract).then_inc(ps.sem, 1)

            def piece_mix(n):
                for i in range(4):
                    vec.wait_ge(piece_pe.sem, piece_pe.at(n, f"mix{i}"))
                    vec.tensor_tensor(carry8[:, 2 * i:2 * i + 2, 0:2 * P], tiles(ep[i % 2], 2),
                                      per_column(bcat[:], 2), ALU.add).then_inc(ps.sem, 1)

            piece_parts = [piece_h, piece_xn, piece_gate, piece_mix]

            def evacuate(g, v, first):
                vec.wait_ge(hi_ready[v % 2], g * (UG // 2) + v // 2 + 1)
                vec.tensor_tensor(turned_lo[v % 2][:], turning0[v % 2], turned_hi[v % 2][:].bitcast(F32),
                                  ALU.subtract).then_inc(lo_ready[v % 2], 1)

            estat = [lstat[:, i, 0:GT] for i in range(10)]
            v1 = carry_in[:, :, P:2 * P]
            hres = carry_in[:, :, 2 * P:3 * P]

            def epi_parts(g):
                es = epi_vec

                def done(name):
                    vec.wait_ge(es.sem, es.at(g, name))

                def gate_pre():
                    vec.wait_ge(carry_loaded, 32 * (g + 1))
                    for t in range(GT):
                        if t % 2 == 0:
                            vec.wait_ge(epi_pe.sem, epi_pe.at(g, ("mix01", "mix23")[t // 2]))
                        ps = ep[t // 2][:, (t % 2) * 2 * P:(t % 2) * 2 * P + P]
                        vec.scalar_tensor_tensor(tiles(fg)[:, t, :], ps, gate[:, bass.ds(g * GT + t, 1)],
                                                 carry_in[:, t, 0:P], ALU.mult, ALU.add).then_inc(es.sem, 1)

                def view2():
                    for t in range(GT):
                        ps = ep[t // 2][:, (t % 2) * 2 * P + P:(t % 2 + 1) * 2 * P]
                        vec.scalar_tensor_tensor(tiles(v2)[:, t, :], ps, gate[:, bass.ds(g * GT + t, 1)],
                                                 ROW["b2"], ALU.mult, ALU.add).then_inc(es.sem, 1)

                def gap():
                    done(f"view2_{GT - 1}")
                    vec.tensor_tensor(tiles(dlt), v1, tiles(v2), ALU.subtract).then_inc(es.sem, 1)
                    vec.wait_ge(epi_act.sem, epi_act.at(g, "exp"))
                    vec.tensor_scalar(fg, fg, 1.0, None, ALU.add).then_inc(es.sem, 1)

                def sigmoid(t):
                    done("one_plus")
                    part = fg[:, t * P:(t + 1) * P]
                    vec.reciprocal(part, part).then_inc(es.sem, 1)

                def fuse():
                    done(f"sigmoid{GT - 1}")
                    vec.tensor_tensor(dlt, dlt, fg, ALU.mult).then_inc(es.sem, 1)
                    done("mixed")
                    vec.tensor_tensor(y, v2, dlt, ALU.add).then_inc(es.sem, 1)

                def resid():
                    done("fused")
                    vec.tensor_tensor(tiles(y), tiles(y), hres, ALU.add).then_inc(es.sem, 1)

                def center_out():
                    done("resid")
                    ln_center(es, g, "out", tiles(y), dlt, estat, GT)

                def norm_out():
                    ln_rstd(es, epi_act, g, "out", estat)
                    vec.tensor_tensor(tiles(y), tiles(dlt), per_tile(estat[9], D), ALU.mult).then_inc(es.sem, 1)

                def scale_out():
                    done("normed")
                    vec.tensor_tensor(tiles(y), tiles(y), per_column(ROW["g_out"], GT), ALU.mult).then_inc(es.sem, 1)
                    done("scaled")
                    vec.tensor_tensor(tiles(y), tiles(y), per_column(ROW["b_out"], GT), ALU.add).then_inc(es.sem, 1)

                def to_x_mid():
                    done("shifted")
                    vec.tensor_tensor(y, y, x_in, ALU.add).then_inc(es.sem, 1)

                def center_next():
                    done("x_mid")
                    ln_center(es, g, "next", tiles(y), dlt, estat, GT)

                def norm_next():
                    ln_rstd(es, epi_act, g, "next", estat)
                    vec.scalar_tensor_tensor(tiles(h1), tiles(dlt), 0.0, per_tile(estat[9], D),
                                             ALU.max, ALU.mult).then_inc(es.sem, 1)

                def heads():
                    vec.wait_ge(epi_pe.sem, epi_pe.at(g, "H"))
                    vec.tensor_tensor(feats[:, bass.ts(g, GT), :], tiles(ep[0]), per_column(ROW["b"], GT),
                                      ALU.add).then_inc(es.sem, 1)
                    vec.wait_ge(epi_pe.sem, epi_pe.at(g, "s"))
                    met(vec)
                    vec.tensor_tensor(s_col[:, bass.ts(g, GT)], ep[2][:, 0:GT], ba[:, 1:2].broadcast_to([P, GT]),
                                      ALU.add).then_inc(es.sem, 1)

                return {2: [gate_pre], 3: [view2], 4: [gap],
                        5: [lambda: sigmoid(0)], 6: [lambda: sigmoid(1)], 7: [lambda: sigmoid(2)],
                        8: [lambda: sigmoid(3)], 9: [fuse], 10: [resid], 11: [center_out],
                        12: [lambda: ln_power(es, epi_act, g, "out", sq, estat, GT)],
                        13: [norm_out], 14: [scale_out], 15: [to_x_mid], 16: [center_next],
                        17: [lambda: ln_power(es, epi_act, g, "next", sq, estat, GT)],
                        18: [norm_next], 22: [heads]}

            for part in piece_parts:
                part(0)
            for c in range(NC):
                for w in range(UC):
                    evacuate(0, c * UC + w, True)
                    if c + 1 < NP:
                        piece_parts[w](c + 1)
            with vec.Fori(1, NG) as g:
                todo = epi_parts(g - 1)
                for v in range(UG):
                    evacuate(g, v, False)
                    for part in todo.get(v, ()):
                        part()
            for parts in epi_parts(NG - 1).values():
                for part in parts:
                    part()

            def score(i, s, c, first):
                half = slot[s][:, c * HALF:(c + 1) * HALF]
                n = 2 * (SLOTS1 * i + s) + c
                vec.wait_ge(half_full[s][c], 16 * (i + 1))
                vec.wait_ge(mask_ready, n + 1)
                vec.scalar_tensor_tensor(half, r_row[:, c * HALF:(c + 1) * HALF], s_col[:, bass.ds(SLOTS1 * i + s, 1)],
                                         half, ALU.add, ALU.mult).then_inc(product_ready, 1)
                vec.wait_ge(product_ready, n + 1)
                vec.scalar_tensor_tensor(half, half, SLOPE, half, ALU.mult, ALU.max).then_inc(leaky_ready, 1)
                vec.wait_ge(leaky_ready, n + 1)
                met(vec)
                vec.tensor_tensor_reduce(half, half, mask[c][:], 1.0, LOWEST, ALU.subtract, ALU.max,
                                         maxes[:, c:c + 1]).then_inc(half_max, 1)

            def row_max(i, s):
                vec.wait_ge(half_max, 2 * (SLOTS1 * i + s) + 2)
                vec.tensor_reduce(top[:], maxes[:], AX.X, ALU.max).then_inc(top_ready, 1)
                vec.wait_ge(top_ready, SLOTS1 * i + s + 1)
                vec.tensor_scalar(negmax[:, s:s + 1], top[:], -1.0 / UNIT, None, ALU.mult).then_inc(max_ready, 1)

            def finish(q, qs):
                fv = fin_vec
                vec.wait_ge(exp_done, 4 * (q + 1))
                vec.tensor_reduce(rinv[:], sums[:, 2 * qs:2 * qs + 2, :], AX.X, ALU.add).then_inc(fv.sem, 1)
                vec.wait_ge(fv.sem, fv.at(q, "total"))
                vec.reciprocal(rinv[:], rinv[:]).then_inc(fv.sem, 1)
                vec.wait_ge(fv.sem, fv.at(q, "rinv"))
                vec.wait_ge(fin_turned, q + 1)
                vec.wait_ge(xm_loaded, 16 * (q + 1))
                vec.tensor_tensor(fin[:], tiles(final[qs], 2), per_tile(rinv[:], P), ALU.mult).then_inc(fv.sem, 1)
                vec.wait_ge(fv.sem, fv.at(q, "scaled"))
                vec.tensor_tensor(fin[:], fin[:], x1_in[:], ALU.add).then_inc(fv.sem, 1)

            def step(i, s, first):
                q = 2 * i + s // 2 - 2
                ends = s % 2 == 0 and not first
                score(i, s, 0, first and s == 0)
                score(i, s, 1, first and s == 0)
                if ends:
                    finish(q, s // 2)
                row_max(i, s)

            vec.wait_ge(epi_act.sem, epi_act.at(NG - 1, "r_row"))
            vec.wait_ge(epi_vec.sem, epi_vec.all(NG))
            for s in range(SLOTS1):
                step(0, s, True)
            with vec.Fori(1, NI) as i:
                for s in range(SLOTS1):
                    step(i, s, False)
            for q in (NQ - 2, NQ - 1):
                finish(q, q % 2)


_INS = ['x', 'adj', 'L0_gnn_u', 'L0_gnn_W1', 'L0_gnn_b1', 'L0_gnn_W2', 'L0_gnn_b2', 'L0_gnn_Wg', 'L0_gnn_bg',
        'L0_gnn_Wn', 'L0_gnn_bn', 'L0_gnn_g_in', 'L0_gnn_b_in', 'L0_gnn_g_out', 'L0_gnn_b_out',
        'L1_gnn_W', 'L1_gnn_b', 'L1_gnn_a_s', 'L1_gnn_a_r']


def kernel(**inputs):
    import numpy as _np
    import concourse.bacc as _bacc
    from concourse import mybir as _mybir
    from concourse.bass_utils import run_bass_kernel_spmd as _run

    nc = _bacc.Bacc("TRN2", target_bir_lowering=False, num_devices=1)
    arrays, args = {}, []
    for name in _INS:
        a = _np.ascontiguousarray(inputs[name])
        arrays[f"in_{name}_dram"] = a
        args.append(nc.dram_tensor(f"in_{name}_dram", a.shape, _mybir.dt.from_np(a.dtype), kind="ExternalInput").ap())
    out = nc.dram_tensor("out_dram", inputs["x"].shape, _mybir.dt.float32, kind="ExternalOutput").ap()
    build(nc, *args, out)
    r = _run(nc, [arrays], core_ids=[0])
    return r.results[0]["out_dram"]
```

```python
from contextlib import ExitStack

import concourse.bass as bass
from concourse import mybir

F32 = mybir.dt.float32
F32R = mybir.dt.float32r
U8 = mybir.dt.uint8
ALU = mybir.AluOpType
ACT = mybir.ActivationFunctionType
AX = mybir.AxisListType

P = 128
BANK = 512
U_FLOOR = 1e-10
LN_EPS = 1e-5
UNIT = 2.0 ** -53
STEEP = -3.0e38
LOWEST = -3.0e38
SLOPE = 0.2
TABLES = "natural_log_exp_and_others"


class Steps:

    def __init__(self, sem, names):
        self.sem, self.names = sem, list(names)
        assert len(set(self.names)) == len(self.names)

    def at(self, n, name):
        return n * len(self.names) + self.names.index(name) + 1

    def all(self, rounds):
        return rounds * len(self.names)


class Stages:

    def __init__(self, sem, kind, stages):
        self.stages = {name: Steps(sem(f"{kind}_{name}"), steps) for name, steps in stages.items()}

    def __getitem__(self, stage):
        return self.stages[stage]

    def at(self, n, step):
        (stage,) = [s for s in self.stages.values() if step in s.names]
        return stage.sem, stage.at(n, step)


def ln_vector_steps(tag):
    return [f"{s}_{tag}" for s in ("sum", "mean", "center", "power", "var", "seed2", "seed2var", "fix", "rstd")]


RSTD_STEPS = ("seed2", "seed2var", "fix", "rstd")


def ln_scalar_steps(tag):
    return [f"{s}_{tag}" for s in ("square", "log", "seed")]


def per_tile(stat, width):
    return stat.unsqueeze(2).broadcast_to([stat.shape[0], stat.shape[1], width])


def per_column(row, tiles):
    return row.unsqueeze(1).broadcast_to([row.shape[0], tiles, row.shape[1]])


def build(nc, x, adj, u, W1, b1, W2, b2, Wg, bg, Wn, bn, g_in, b_in, g_out, b_out, W, b, a_s, a_r, out):
    N, D = x.shape
    NT = N // P
    GT = 4
    NG = NT // GT
    CW = 1024
    NC = N // CW
    SLOTS0 = 3
    UB = 2
    UC = CW // P // UB
    UG = NC * UC
    PW = GT * P
    PTL = CW // P
    NP = NT // PTL
    HALF = N // 2
    SLOTS1 = 4
    LW = 1024
    VB = 4
    VU = NT // VB
    LOADS = (((0, 3), (3, 6)), ((6, 9), (9, 10), (10, 11), (11, 12)))
    NQ = NT // 2
    NI = NT // SLOTS1
    CONSTS = 17
    assert D == P and NC % SLOTS0 == 0 and UG % 2 == 0 and NP == NC and VU == 12 and NC * CW == N

    with ExitStack() as ctx:
        def sb(name, shape, dt=F32):
            return ctx.enter_context(nc.sbuf_tensor(name, shape, dt))

        def sem(name):
            return ctx.enter_context(nc.semaphore(name))

        feats = sb("feats", [P, NT, D])
        r_row = sb("r_row", [P, N])
        s_col = sb("s_col", [P, NT])
        gate = sb("gate", [P, NT])
        ident = sb("ident", [P, P])
        wcat = sb("wcat", [P, 2, 2 * P])
        wn_sb = sb("wn_sb", [P, 2])
        wT = sb("wT", [P, P])
        wraw = sb("wraw", [P, P])
        bcat = r_row[:, 3 * P:5 * P]
        bcat_hi = sb("bcat_hi", [P, 4 * P], F32R)
        bcat_lo = sb("bcat_lo", [P, 4 * P], F32R)
        one_row = r_row[:, 0:P]
        one_row_r = sb("one_row_r", [P, P], F32R)
        rows = sb("rows", [P, 6, P])
        ROW = {n: rows[:, i, :] for i, n in enumerate(("b2", "g_in", "b_in", "g_out", "b_out", "b"))}
        vecs = sb("vecs", [P, 3])
        a_wide = sb("a_wide", [P, P + 1])
        b_wide = sb("b_wide", [P, P])
        wa = sb("wa", [P, P + 1])
        ba = sb("ba", [P, 2])
        bn_row = sb("bn_row", [P, 2])
        noise = sb("noise", [P, NT, 2])
        lstat = sb("lstat", [P, 2, 10, PTL])
        zbuf = sb("zbuf", [P, 2, PTL, 2])
        zstat = sb("zstat", [P, 6, PTL])
        eps = sb("eps", [P, 2])
        s08_col = sb("s08_col", [P, NT])
        s02_col = sb("s02_col", [P, NT])
        r_parts = sb("r_parts", [P, LW], F32R)
        pick = r_row[:, P:3 * P].rearrange("p (c i) -> p c i", c=2)
        pick_r = sb("pick_r", [P, 2, P], F32R)
        ones = sb("ones", [P, 1])

        def tiles(a, n=GT):
            return a[:].rearrange("p (t d) -> p t d", t=n)

        with ExitStack() as l0:
            def sb0(name, shape, dt=F32):
                return l0.enter_context(nc.sbuf_tensor(name, shape, dt))

            ring_mem = sb0("ring_mem", [P, SLOTS0 * GT * CW])
            ring = [ring_mem[:, s * GT * CW:(s + 1) * GT * CW].rearrange("p (t c) -> p t c", t=GT)
                    for s in range(SLOTS0)]
            gated_hi = sb0("gated_hi", [P, NT, D], F32R)
            gated_lo = sb0("gated_lo", [P, NT, D], F32R)
            turned_hi = [sb0(f"turned_hi{i}", [P, UB * PW], F32R) for i in range(2)]
            turned_lo = [sb0(f"turned_lo{i}", [P, UB * PW], F32R) for i in range(2)]
            PX = PTL * D
            scratch = sb0("scratch", [P, 7 * PX])
        x8 = [scratch[:, i * PX:(i + 1) * PX] for i in range(2)]
        xn8 = [scratch[:, i * PX:(i + 1) * PX] for i in (2, 3)]
        c1_8 = scratch[:, 4 * PX:6 * PX]
        xnT8 = scratch[:, 6 * PX:7 * PX]
        cx8, sqx8, h8, ch8, sqh8 = (feats[:, i * PTL:(i + 1) * PTL, :].rearrange("p t d -> p (t d)") for i in range(5))
        carry_in = tiles(scratch[:, 0:GT * 3 * P])
        e0 = GT * 3 * P
        x_in, rawT, fg, v2, dlt, y, sq, h1, h1T = (scratch[:, e0 + i * PW:e0 + (i + 1) * PW] for i in range(9))
        assert e0 + 9 * PW <= 7 * PX
        stage = sb("stage", [P, SLOTS1 * N])
        slot = [stage[:, s * N:(s + 1) * N] for s in range(SLOTS1)]
        mask = [sb(f"mask{i}", [P, HALF], U8) for i in range(2)]
        probT = [sb(f"probT{i}", [P, VB * 2 * P]) for i in range(2)]
        maxes = sb("maxes", [P, SLOTS1, 2])
        top = sb("top", [P, 1])
        negmax = sb("negmax", [P, SLOTS1])
        sums = sb("sums", [P, SLOTS1, 2])
        rinv = sb("rinv", [P, 2])
        oT = sb("oT", [P, 2 * P])
        x1_in = sb("x1_in", [P, 2, P])
        fin = sb("fin", [P, 2, P])

        pstat = [[lstat[:, i, k, :] for k in range(10)] for i in range(2)]
        estat = [lstat[:, 0, k, 0:GT] for k in range(10)]

        psum = ctx.enter_context(nc.psum_tensor("psum", [P, 8 * BANK], F32))

        def bank(i, n=1):
            return psum[:, i * BANK:(i + n) * BANK]

        turning0 = [bank(0, 2), bank(2, 2)]
        acc0 = bank(4)
        ep = [bank(5), bank(6), bank(7)]
        leaky = bank(2, 2)
        turning1 = [bank(0, 2), bank(4, 2)]
        acc1 = [bank(6)[:, 0:2 * P], bank(7)[:, 0:2 * P]]
        final = [bank(6)[:, 2 * P:4 * P], bank(7)[:, 2 * P:4 * P]]

        carry = nc.dram_tensor("carry", (N, 3 * P), F32, kind="Internal").ap()
        x_mid = nc.dram_tensor("x_mid", (N, D), F32, kind="Internal").ap()

        def by_tile(a):
            return a.rearrange("(t p) d -> p t d", p=P)

        consts_in = sem("consts_in")
        noise_in = sem("noise_in")
        x_loaded = [sem("x_loaded0"), sem("x_loaded1")]
        ident_ready = sem("ident_ready")
        noise_vec = Steps(sem("noise_vec"), ["eps_log", "eps_ln", "one", "clipped", "bias"])
        noise_act = Steps(sem("noise_act"), ["log", "loglog"])
        wT_turned = sem("wT_turned")
        attend = Steps(sem("attend"), ["a_s", "a_r", "b", "wT", "wa", "ba"])
        bias_ready = sem("bias_ready")
        LEAD = 12
        piece_vec = Stages(sem, "piece_vec", {
            "center_x": ["sum_x", "mean_x", "center_x"], "power_x": ["power_x", "var_x"],
            "h": [*(f"{s}_x" for s in RSTD_STEPS), "h"], "center_h": ["sum_h", "mean_h", "center_h"],
            "power_h": ["power_h", "var_h"], "rstd_h": [f"{s}_h" for s in RSTD_STEPS], "xn": ["scaled", "xn"],
            "z": ["z", "zmax", "zsub"], "gate": ["esum", "erec", "p1", "hard", "y", "gate"],
            "gated": ["gated"], "lo": ["lo"]})
        piece_act = Stages(sem, "piece_act", {
            "square_x": ["square_x"], "seed_x": ["log_x", "seed_x"], "square_h": ["square_h"],
            "seed_h": ["log_h", "seed_h"], "normed": [f"normed{t}" for t in range(PTL)],
            "xnT": ["xnT0", "xnT1"], "exp": ["exp"], "mix": [f"mix{i}" for i in range(4)],
            "hi": ["hi"]})
        piece_pe = Stages(sem, "piece_pe", {
            "turn": ["turn0", "turn1"], "logits": ["logits"], "mix": [f"mix{i}" for i in range(4)]})
        h_stored, c1_stored = sem("h_stored"), sem("c1_stored")

        def due(parts, v):
            return [(parts[v + LEAD - UC * n], n) for n in range(NP) if v + LEAD - UC * n in parts]

        chunk_full = [sem(f"chunk_full{s}") for s in range(SLOTS0)]
        blocks_turned = sem("blocks_turned")
        lo_ready = [sem("lo_ready0"), sem("lo_ready1")]
        hi_ready = [sem("hi_ready0"), sem("hi_ready1")]
        unit_summed = sem("unit_summed")
        acc_copied = sem("acc_copied")
        epi_vec = Steps(sem("epi_vec"), [
            *(f"gpre{t}" for t in range(GT)), *(f"view2_{t}" for t in range(GT)),
            "gap", "one_plus", *(f"sigmoid{t}" for t in range(GT)), "mixed", "fused", "resid",
            *ln_vector_steps("out"), "normed", "scaled", "shifted", "x_mid",
            *ln_vector_steps("next"), "h1", "H", "s", "s08", "s02"])
        epi_act = Steps(sem("epi_act"), ["exp", *ln_scalar_steps("out"), *ln_scalar_steps("next"), "h1T", "r_row"])
        epi_pe = Steps(sem("epi_pe"), ["mix01", "mix23", "turn", "H", "s", "r_row"])
        carry_loaded = sem("carry_loaded")
        x_mid_stored = sem("x_mid_stored")
        half_full = [[sem(f"half_full{s}_{c}") for c in range(2)] for s in range(SLOTS1)]
        r_hi_ready, r_lo_ready = sem("r_hi_ready"), sem("r_lo_ready")
        leaky_opened = sem("leaky_opened")
        relu_ready = sem("relu_ready")
        w_ready = sem("w_ready")
        mask_ready = sem("mask_ready")
        sums_copied = sem("sums_copied")
        score_vec = Steps(sem("score_vec"), ["product", "from_psum", "leaky"])
        half_max = sem("half_max")
        top_ready, max_ready = sem("top_ready"), sem("max_ready")
        exp_done = sem("exp_done")
        probs_turned = sem("probs_turned")
        probT_ready = [sem("probT_ready0"), sem("probT_ready1")]
        probs_summed = sem("probs_summed")
        fin_vec = Steps(sem("fin_vec"), ["total", "rinv", "scaled", "out"])
        fin_turned = sem("fin_turned")
        xm_loaded = sem("xm_loaded")
        out_stored = sem("out_stored")

        waits_met = sem("waits_met")

        def met(engine):
            engine.sem_inc(waits_met, 1)

        def at_slot(i, s):
            return i + s // SLOTS1, s % SLOTS1

        def nth(i, s, c):
            if isinstance(i, int) and i == 0 and s < 2:
                return s + 2 * c
            return 2 * (SLOTS1 * i + s) + c

        block = ctx.enter_context(nc.Block())

        @block.sync
        def _(sp):
            def load_piece(n):
                if n >= 2:
                    sp.wait_ge(*piece_vec.at(n - 2, "center_x"))
                sp.dma_start(tiles(x8[n % 2], PTL), by_tile(x)[:, n * PTL:(n + 1) * PTL, :]).then_inc(x_loaded[n % 2], 16)

            def store_h(n):
                sp.wait_ge(*piece_vec.at(n, "h"))
                sp.dma_start(by_tile(carry)[:, n * PTL:(n + 1) * PTL, 2 * P:3 * P], tiles(h8, PTL)).then_inc(h_stored, 16)

            def store_c1(n):
                sp.wait_ge(*piece_act.at(n, "mix3"))
                sp.dma_start(by_tile(carry)[:, n * PTL:(n + 1) * PTL, 0:2 * P], tiles(c1_8, PTL)).then_inc(c1_stored, 16)

            adj_groups = adj.rearrange("(g t p) c -> g p t c", t=GT, p=P)

            def load_chunk(g, c, first):
                s = c % SLOTS0
                if not (first and c < SLOTS0):
                    sp.wait_ge(blocks_turned, g * UG + (c - SLOTS0 + 1) * UC)
                sp.dma_start(ring[s], adj_groups[g, :, :, c * CW:(c + 1) * CW]).then_inc(chunk_full[s], 16)

            def load_carry(g):
                sp.wait_ge(x_mid_stored, 16 * g)
                fetch_carry(g)

            def fetch_carry(g):
                sp.dma_start(carry_in, by_tile(carry)[:, bass.ts(g, GT), :]).then_inc(carry_loaded, 16)
                sp.dma_start(tiles(x_in), by_tile(x)[:, bass.ts(g, GT), :]).then_inc(carry_loaded, 16)

            def store_x_mid(g):
                sp.wait_ge(epi_vec.sem, epi_vec.at(g, "x_mid"))
                sp.dma_start(by_tile(x_mid)[:, bass.ts(g, GT), :], tiles(y)).then_inc(x_mid_stored, 16)

            load_piece(0)
            for src, dst in ((u.rearrange("(t p) k -> p t k", p=P), noise[:]),
                             (bn.partition_broadcast(P), bn_row[:])):
                sp.dma_start(dst, src).then_inc(noise_in, 16)
            for src, dst in ((Wg[0:P, :], wcat[:, 0, 0:P]), (W1, wcat[:, 0, P:2 * P]),
                             (Wg[P:2 * P, :], wcat[:, 1, 0:P]), (W2, wcat[:, 1, P:2 * P]),
                             (Wn, wn_sb[:]), (W, wraw[:]),
                             (bg.partition_broadcast(P), bcat[:, 0:P]), (b1.partition_broadcast(P), bcat[:, P:2 * P]),
                             (b2.partition_broadcast(P), ROW["b2"]), (g_in.partition_broadcast(P), ROW["g_in"]),
                             (b_in.partition_broadcast(P), ROW["b_in"]), (g_out.partition_broadcast(P), ROW["g_out"]),
                             (b_out.partition_broadcast(P), ROW["b_out"]), (b.partition_broadcast(P), ROW["b"]),
                             (a_s, vecs[:, 0:1]), (a_r, vecs[:, 1:2]),
                             (b.rearrange("(d k) -> d k", k=1), vecs[:, 2:3])):
                sp.dma_start(dst, src).then_inc(consts_in, 16)
            load_piece(1)
            for m in range(-2, NP):
                if 2 <= m + 4 < NP:
                    load_piece(m + 4)
                if m + 2 < NP:
                    store_h(m + 2)
                if m >= 0:
                    store_c1(m)
                for c in {-2: [0], -1: [1, 2], 0: []}.get(m, [m + 2] if m + 2 < NC else []):
                    load_chunk(0, c, True)
            sp.wait_ge(h_stored, 16 * NP)
            sp.wait_ge(c1_stored, 16 * NP)
            fetch_carry(0)
            with sp.Fori(1, NG) as g:
                for c in range(NC):
                    load_chunk(g, c, False)
                store_x_mid(g - 1)
                load_carry(g)

            adj_tiles = adj.rearrange("(t p) c -> t p c", p=P)

            def load_units(k, s, v, w):
                cols = slice(v * VB * P, w * VB * P)
                sp.dma_start(slot[s][:, cols], adj_tiles[k, :, cols]).then_inc(half_full[s][v // (VU // 2)], 16)

            def load_half(k, s, c):
                for v, w in LOADS[c]:
                    load_units(k, s, v, w)

            sp.wait_ge(blocks_turned, NG * UG)
            for c in range(2):
                for s in range(2):
                    load_half(s, s, c)
            sp.wait_ge(unit_summed, NG * UG)
            for s in range(2, SLOTS1):
                for c in range(2):
                    load_half(s, s, c)
            store_x_mid(NG - 1)
            sp.wait_ge(x_mid_stored, 16 * NG)

            def load_x_mid(q):
                sp.dma_start(x1_in[:], by_tile(x_mid)[:, bass.ts(q, 2), :]).then_inc(xm_loaded, 16)

            def store_out(q):
                sp.wait_ge(fin_vec.sem, fin_vec.at(q, "out"))
                sp.dma_start(by_tile(out)[:, bass.ts(q, 2), :], fin[:]).then_inc(out_stored, 16)

            def next_pair(i, q, first=False):
                before = 2 * i + q - 2
                for c in range(2):
                    for v, w in LOADS[c]:
                        sp.wait_ge(probs_turned, before * VU + w)
                        for s in (2 * q, 2 * q + 1):
                            load_units(SLOTS1 * i + s, s, v, w)
                if not first:
                    store_out(before - 1)
                load_x_mid(before)

            next_pair(1, 0, first=True)
            next_pair(1, 1)
            with sp.Fori(2, NI) as i:
                next_pair(i, 0)
                next_pair(i, 1)
            for q in (NQ - 2, NQ - 1):
                store_out(q - 1)
                load_x_mid(q)
            store_out(NQ - 1)
            sp.wait_ge(out_stored, 16 * NQ)

        @block.gpsimd
        def _(pool):
            pool.memset(ident[:], 0.0).then_inc(ident_ready, 1)
            pool.wait_ge(ident_ready, 1)
            pool.affine_select(out=ident[:], in_=ident[:], compare_op=ALU.not_equal, fill=1.0, base=0,
                               pattern=[[-1, P]], channel_multiplier=1).then_inc(ident_ready, 1)
            pool.memset(one_row, 0.0).then_inc(ident_ready, 1)
            pool.wait_ge(ident_ready, 3)
            pool.memset(one_row[0:1, :], 1.0).then_inc(ident_ready, 1)
            pool.memset(pick, 0.0).then_inc(ident_ready, 1)
            pool.wait_ge(ident_ready, 5)
            for c in range(2):
                for part in range(2):
                    row = 64 * c + 32 * part
                    pool.memset(pick[row:row + 1, c, :], 1.0).then_inc(ident_ready, 1)

        @block.scalar
        def _(act):
            def ln_square(steps, vec, n, tag, src, dst):
                act.wait_ge(vec.sem, vec.at(n, f"center_{tag}"))
                act.activation(dst, src, ACT.Square).then_inc(steps.sem, 1)

            def ln_seed(steps, vec, n, tag, stat):
                act.wait_ge(vec.sem, vec.at(n, f"power_{tag}"))
                act.activation(stat[3], stat[2], ACT.Ln, scale=1.0 / D, bias=eps[:, 0:1]).then_inc(steps.sem, 1)
                act.wait_ge(steps.sem, steps.at(n, f"log_{tag}"))
                act.activation(stat[4], stat[3], ACT.Exp, scale=-0.5).then_inc(steps.sem, 1)

            act.preload_act_table_set(TABLES)
            act.wait_ge(noise_vec.sem, noise_vec.at(0, "one"))

            def gumbel():
                act.wait_ge(noise_vec.sem, noise_vec.at(0, "clipped"))
                act.activation(noise[:], noise[:], ACT.Ln).then_inc(noise_act.sem, 1)
                act.wait_ge(noise_act.sem, noise_act.at(0, "log"))
                act.activation(noise[:], noise[:], ACT.Ln, scale=-1.0, bias=eps[:, 1:2]).then_inc(noise_act.sem, 1)

            def piece_square_x(n):
                ln_square(piece_act["square_x"], piece_vec["center_x"], n, "x", cx8, sqx8)

            def piece_seed_x(n):
                ln_seed(piece_act["seed_x"], piece_vec["power_x"], n, "x", pstat[0])

            def piece_square_h(n):
                ln_square(piece_act["square_h"], piece_vec["center_h"], n, "h", ch8, sqh8)

            def piece_seed_h(n):
                ln_seed(piece_act["seed_h"], piece_vec["power_h"], n, "h", pstat[1])

            def piece_normed(n):
                act.wait_ge(*piece_vec.at(n, "rstd_h"))
                if n >= 2:
                    act.wait_ge(*piece_vec.at(n - 2, "lo"))
                for t in range(PTL):
                    act.activation(tiles(xn8[n % 2], PTL)[:, t, :], tiles(ch8, PTL)[:, t, :], ACT.Copy,
                                   scale=pstat[1][9][:, t:t + 1]).then_inc(piece_act["normed"].sem, 1)

            def piece_turned(n):
                for i in range(2):
                    act.wait_ge(*piece_pe.at(n, f"turn{i}"))
                    if n >= 1:
                        act.wait_ge(*piece_pe.at(n - 1, "mix3"))
                    act.activation(xnT8[:, i * BANK:(i + 1) * BANK], ep[i], ACT.Copy).then_inc(piece_act["xnT"].sem, 1)

            def piece_mixed(n, these):
                for i in these:
                    act.wait_ge(*piece_pe.at(n, f"mix{i}"))
                    if i == 0 and n >= 1:
                        act.wait_ge(c1_stored, 16 * n)
                    act.activation(c1_8[:, i * BANK:(i + 1) * BANK], ep[i % 2], ACT.Copy).then_inc(piece_act["mix"].sem, 1)

            def piece_exp(n):
                act.wait_ge(*piece_vec.at(n, "zsub"))
                act.activation(zbuf[:, 1], zbuf[:, 0], ACT.Exp).then_inc(piece_act["exp"].sem, 1)
                piece_mixed(n, (1, 2))

            def piece_hi(n):
                act.wait_ge(*piece_vec.at(n, "gated"))
                act.activation(gated_hi[:, n * PTL:(n + 1) * PTL, :], tiles(xn8[n % 2], PTL),
                               ACT.Copy).then_inc(piece_act["hi"].sem, 1)

            piece_parts = {1: piece_square_x, 2: piece_seed_x, 4: piece_square_h, 5: piece_seed_h, 6: piece_normed,
                           8: piece_turned, 9: lambda n: piece_mixed(n, (0,)), 10: piece_exp,
                           11: lambda n: piece_mixed(n, (3,)), 12: piece_hi}

            def evacuate(g, v, first):
                n = g * UG + v
                act.wait_ge(blocks_turned, n + 1)
                if not (first and v < 2):
                    act.wait_ge(unit_summed, n - 1)
                act.activation(turned_hi[v % 2][:], turning0[v % 2], ACT.Copy).then_inc(hi_ready[v % 2], 1)

            def copy_acc(g):
                act.wait_ge(unit_summed, (g + 1) * UG)
                act.activation(rawT, acc0, ACT.Copy).then_inc(acc_copied, 1)

            def epi_exp(g):
                act.wait_ge(epi_vec.sem, epi_vec.at(g, f"gpre{GT - 1}"))
                act.activation(fg, fg, ACT.Exp, scale=-1.0).then_inc(epi_act.sem, 1)

            def epi_turn(g):
                act.wait_ge(epi_pe.sem, epi_pe.at(g, "turn"))
                act.activation(h1T, ep[2], ACT.Copy).then_inc(epi_act.sem, 1)

            def epi_r(g):
                act.wait_ge(epi_pe.sem, epi_pe.at(g, "r_row"))
                act.activation(r_row[:, bass.ts(g, PW)], ep[1], ACT.Identity, bias=ba[:, 0:1]).then_inc(epi_act.sem, 1)

            def epilogue(g):
                return {3: [lambda: epi_exp(g)],
                        12: [lambda: ln_square(epi_act, epi_vec, g, "out", dlt, sq)],
                        13: [lambda: ln_seed(epi_act, epi_vec, g, "out", estat)],
                        17: [lambda: ln_square(epi_act, epi_vec, g, "next", dlt, sq)],
                        18: [lambda: ln_seed(epi_act, epi_vec, g, "next", estat)],
                        21: [lambda: epi_turn(g)],
                        23: [lambda: epi_r(g)]}

            for v in range(-LEAD, UG):
                if v >= 0:
                    evacuate(0, v, True)
                if v == 3 - LEAD:
                    gumbel()
                for part, n in due(piece_parts, v):
                    part(n)
            with act.Fori(1, NG) as g:
                todo = epilogue(g - 1)
                for v in range(UG):
                    evacuate(g, v, False)
                    if v == 0:
                        copy_acc(g - 1)
                    for f in todo.get(v, []):
                        f()
            act.wait_ge(epi_act.sem, epi_act.at(NG - 2, "r_row"))
            for c in range(2):
                act.activation(r_parts[64 * c:64 * c + 64, :], r_row[64 * c:64 * c + 64, c * HALF:c * HALF + LW],
                               ACT.Copy, scale=SLOPE).then_inc(r_hi_ready, 1)
            copy_acc(NG - 1)

            def relus(i, s, c):
                i, s = at_slot(i, s)
                n = nth(i, s, c)
                act.wait_ge(leaky_opened, n + 1)
                met(act)
                act.activation(leaky, r_row[:, c * HALF:c * HALF + LW], ACT.Relu, scale=1.0 - SLOPE,
                               bias=s08_col[:, bass.ds(SLOTS1 * i + s, 1)]).then_inc(relu_ready, 1)

            def masks(i, s, c):
                i, s = at_slot(i, s)
                n = nth(i, s, c)
                act.wait_ge(half_full[s][c], 16 * len(LOADS[c]) * (i + 1))
                if not (isinstance(n, int) and n < 2):
                    act.wait_ge(half_max, n - 1)
                buf = n % 2 if isinstance(n, int) else c
                act.activation(mask[buf][:], slot[s][:, c * HALF:(c + 1) * HALF], ACT.Relu,
                               scale=STEEP, bias=ones[:]).then_inc(mask_ready, 1)

            def exps(i, s, c, first):
                i, s = at_slot(i, s)
                act.wait_ge(max_ready, SLOTS1 * i + s + 1)
                if c == 0 and not first:
                    act.wait_ge(fin_vec.sem, fin_vec.at(2 * i + s // 2 - 2, "total"))
                half = slot[s][:, c * HALF:(c + 1) * HALF]
                act.activation(half, half, ACT.Exp, bias=negmax[:, s:s + 1], scale=1.0 / UNIT,
                               accum_out=sums[:, s, c:c + 1]).then_inc(exp_done, 1)

            def evacuate1(i, s, v, first):
                i, s = at_slot(i, s)
                n = (2 * i + s // 2) * VU + v
                act.wait_ge(probs_turned, n + 1)
                if not (first and v < 2):
                    act.wait_ge(probs_summed, n - 1)
                act.activation(probT[v % 2][:], turning1[v % 2], ACT.Copy).then_inc(probT_ready[v % 2], 1)

            def copy_sums(q, qs):
                act.wait_ge(probs_summed, VU * (q + 1))
                if not (isinstance(q, int) and q == 0):
                    act.wait_ge(fin_turned, q)
                act.activation(oT[:], acc1[qs], ACT.Copy).then_inc(sums_copied, 1)

            def step(i, s, start=False, fresh=False, last=False, here=True):
                for c in range(2):
                    base = (2 * (s % 2) + c) * VU // 4
                    exps(i, s - 1, c, start or fresh)
                    if not (start and s == 2 and base == 0):
                        evacuate1(i, s - 2, base - 1, start and s == 2)
                    ahead = (i, s + c, 1 - c) if (here if c == 0 else not last) else None
                    if ahead:
                        masks(*ahead)
                    evacuate1(i, s - 2, base, start and s == 2)
                    if ahead:
                        relus(*ahead)
                    evacuate1(i, s - 2, base + 1, start and s == 2)
                    if base == 0 and not start:
                        j, t = at_slot(i, s - 4)
                        copy_sums(2 * j + t // 2, t // 2)

            tail = epilogue(NG - 1)

            def ends(v):
                for part in tail[v]:
                    part()

            ends(3)
            relus(0, 0, 0)
            masks(0, 0, 0)
            ends(12)
            ends(13)
            masks(0, 1, 0)
            masks(0, 0, 1)
            ends(17)
            relus(0, 1, 0)
            ends(18)
            relus(0, 0, 1)
            ends(21)
            ends(23)
            act.wait_ge(epi_vec.sem, epi_vec.all(NG))
            act.wait_ge(epi_pe.sem, epi_pe.all(NG))
            masks(0, 1, 1)
            relus(0, 1, 1)
            exps(0, 0, 0, True)
            masks(0, 2, 0)
            relus(0, 2, 0)
            exps(0, 0, 1, True)
            for s in range(2, SLOTS1):
                step(0, s, start=True)
            step(1, 0, fresh=True)
            with act.Fori(1, NI - 1) as i:
                for s in range(1, SLOTS1 + 1):
                    step(*at_slot(i, s))
            for s in range(1, SLOTS1 + 1):
                step(NI - 1, s, last=s >= SLOTS1 - 1, here=s < SLOTS1)
            for v in range(VU // 2 - 1, VU):
                evacuate1(NI - 1, 2, v, False)
            copy_sums(NQ - 1, 1)

        @block.tensor
        def _(pe):
            pe.wait_ge(ident_ready, 4)
            pe.wait_ge(consts_in, 16 * CONSTS)
            pe.transpose(ep[2][:, P:2 * P], wraw[:], ident[:])
            pe.wait_ge(attend.sem, attend.at(0, "b"))
            pe.matmul(ep[1][:, 0:P + 1], wraw[:], a_wide[:], start=True, stop=True)
            pe.matmul(ep[1][:, P + 1:P + 3], b_wide[:], a_wide[:, P - 1:P + 1], start=True,
                      stop=True).then_inc(wT_turned, 1)

            def piece_turn(n):
                pe.wait_ge(*piece_vec.at(n, "xn"))
                if n == 0:
                    pe.wait_ge(attend.sem, attend.all(1))
                else:
                    pe.wait_ge(*piece_act.at(n - 1, "mix3"))
                for i in range(2):
                    for t in range(4):
                        mm = pe.transpose(ep[i][:, t * P:(t + 1) * P], tiles(xn8[n % 2], PTL)[:, 4 * i + t, :], ident[:])
                    mm.then_inc(piece_pe["turn"].sem, 1)

            def piece_mix(n, these):
                if n == 0:
                    pe.wait_ge(bias_ready, 4)
                for i in these:
                    pe.wait_ge(*piece_act.at(n, f"mix{i - 2}" if i >= 2 else "xnT1"))
                    pe.matmul(ep[i % 2], one_row_r[:], bcat_hi[:], start=True, stop=False)
                    pe.matmul(ep[i % 2], one_row_r[:], bcat_lo[:], start=False, stop=False)
                    for t in range(2):
                        mm = pe.matmul(ep[i % 2][:, t * 2 * P:(t + 1) * 2 * P], xnT8[:, (2 * i + t) * P:(2 * i + t + 1) * P],
                                       wcat[:, 0, :], start=False, stop=t == 1)
                    mm.then_inc(piece_pe["mix"].sem, 1)

            def piece_logits(n):
                pe.wait_ge(*piece_act.at(n, "xnT1"))
                if n >= 1:
                    pe.wait_ge(*piece_vec.at(n - 1, "z"))
                for t in range(PTL):
                    mm = pe.matmul(ep[2][:, 2 * t:2 * t + 2], xnT8[:, t * P:(t + 1) * P], wn_sb[:], start=True, stop=True)
                mm.then_inc(piece_pe["logits"].sem, 1)
                piece_mix(n, (0,))

            piece_parts = {7: piece_turn, 8: piece_logits, 9: lambda n: piece_mix(n, (1, 2)),
                           10: lambda n: piece_mix(n, (3,))}

            def turn(g, v, first):
                n = g * UG + v
                c, w = v // UC, v % UC
                s = c % SLOTS0
                if w == 0:
                    pe.wait_ge(chunk_full[s], 16 * (g * (NC // SLOTS0) + c // SLOTS0 + 1))
                if not (first and v < 2):
                    pe.wait_ge(lo_ready[v % 2], g * (UG // 2) + v // 2)
                for j in range(UB):
                    for t in range(GT):
                        mm = pe.transpose(turning0[v % 2][:, j * PW + t * P:j * PW + (t + 1) * P],
                                          ring[s][:, t, (w * UB + j) * P:(w * UB + j + 1) * P], ident[:])
                mm.then_inc(blocks_turned, 1)

            def gather(g, v, first):
                if first and v % UC == 0:
                    pe.wait_ge(*piece_vec.at(v // UC, "lo"))
                if v == 0 and not first:
                    pe.wait_ge(acc_copied, g)
                pe.wait_ge(hi_ready[v % 2], g * (UG // 2) + v // 2 + 1)
                def product(j, gated, turned, **ends):
                    return pe.matmul(acc0, gated[:, v * UB + j, :], turned[v % 2][:, j * PW:(j + 1) * PW], **ends)

                for j in range(UB):
                    product(j, gated_hi, turned_hi, start=v == 0 and j == 0, stop=False)
                    product(j, gated_lo, turned_hi, start=False, stop=False)
                pe.wait_ge(lo_ready[v % 2], g * (UG // 2) + v // 2 + 1)
                for j in range(UB):
                    mm = product(j, gated_hi, turned_lo, start=False, stop=v == UG - 1 and j == UB - 1)
                mm.then_inc(unit_summed, 1)

            def epi_mix(g, i):
                if i == 0:
                    pe.wait_ge(acc_copied, g + 1)
                    pe.wait_ge(*piece_act.at(NP - 1, "mix3"))
                    pe.wait_ge(*piece_vec.at(NP - 1, "z"))
                for t in range(2):
                    mm = pe.matmul(ep[i][:, t * 2 * P:(t + 1) * 2 * P], rawT[:, (2 * i + t) * P:(2 * i + t + 1) * P],
                                   wcat[:, 1, :], start=True, stop=True)
                mm.then_inc(epi_pe.sem, 1)

            def epi_turn(g):
                pe.wait_ge(epi_vec.sem, epi_vec.at(g, "h1"))
                for t in range(GT):
                    mm = pe.transpose(ep[2][:, t * P:(t + 1) * P], h1[:, t * P:(t + 1) * P], ident[:])
                mm.then_inc(epi_pe.sem, 1)

            def epi_h(g):
                pe.wait_ge(epi_act.sem, epi_act.at(g, "h1T"))
                for t in range(GT):
                    mm = pe.matmul(ep[0][:, t * P:(t + 1) * P], h1T[:, t * P:(t + 1) * P], wT[:], start=True, stop=True)
                mm.then_inc(epi_pe.sem, 1)
                for t in range(GT):
                    mm = pe.matmul(ep[2][:, t:t + 1], h1T[:, t * P:(t + 1) * P], wa[:, P:P + 1], start=True, stop=True)
                mm.then_inc(epi_pe.sem, 1)

            def epi_r(g):
                pe.matmul(ep[1], wa[:, 0:P], h1T, start=True, stop=True).then_inc(epi_pe.sem, 1)

            def epilogue(g):
                return {0: [lambda: epi_mix(g, 0)], 1: [lambda: epi_mix(g, 1)], 19: [lambda: epi_turn(g)],
                        21: [lambda: epi_h(g)], 22: [lambda: epi_r(g)]}

            for v in range(-LEAD, UG):
                if v >= 0:
                    turn(0, v, True)
                if v >= 1:
                    gather(0, v - 1, True)
                for part, n in due(piece_parts, v):
                    part(n)
            with pe.Fori(1, NG) as g:
                todo = epilogue(g - 1)
                for v in range(UG):
                    turn(g, v, False)
                    if v == 0:
                        gather(g - 1, UG - 1, False)
                    else:
                        gather(g, v - 1, False)
                    for f in todo.get(v - 1, []):
                        f()
            gather(NG - 1, UG - 1, False)

            def open_leaky(n):
                if isinstance(n, int) and n == 0:
                    pe.wait_ge(lo_ready[1], NG * (UG // 2))
                    pe.wait_ge(r_lo_ready, 2)
                else:
                    pe.wait_ge(score_vec.sem, score_vec.at(n - 1, "from_psum"))
                for k in range(LW // BANK):
                    cols = slice(k * BANK, (k + 1) * BANK)
                    mm = pe.matmul(leaky[:, cols], pick_r[:, 0, :], r_parts[:, cols], start=True, stop=False)
                mm.then_inc(leaky_opened, 1)

            def add_r(n, c):
                pe.wait_ge(relu_ready, n + 1)
                for k in range(LW // BANK):
                    cols = slice(k * BANK, (k + 1) * BANK)
                    mm = pe.matmul(leaky[:, cols], pick_r[:, c, :], r_parts[:, cols], start=False, stop=True)
                mm.then_inc(w_ready, 1)

            open_leaky(0)
            epi_mix(NG - 1, 0)
            epi_mix(NG - 1, 1)
            add_r(0, 0)
            open_leaky(1)
            add_r(1, 0)
            open_leaky(2)
            epi_turn(NG - 1)
            epi_h(NG - 1)
            add_r(2, 1)
            epi_r(NG - 1)
            for n, c in ((3, 1), (4, 0)):
                open_leaky(n)
                add_r(n, c)

            def turn1(q, qs, v, first):
                c = v // (VU // 2)
                if v % (VU // 2) == 0:
                    pe.wait_ge(exp_done, 2 * (2 * q + 1) + c + 1)
                if not (first and v < 2):
                    pe.wait_ge(probT_ready[v % 2], q * (VU // 2) + v // 2)
                for j in range(VB):
                    for t in range(2):
                        mm = pe.transpose(turning1[v % 2][:, (2 * j + t) * P:(2 * j + t + 1) * P],
                                          slot[2 * qs + t][:, (v * VB + j) * P:(v * VB + j + 1) * P], ident[:])
                mm.then_inc(probs_turned, 1)

            def gather1(q, qs, v):
                pe.wait_ge(probT_ready[v % 2], q * (VU // 2) + v // 2 + 1)
                for j in range(VB):
                    blk = v * VB + j
                    mm = pe.matmul(acc1[qs], feats[:, blk, :], probT[v % 2][:, j * 2 * P:(j + 1) * 2 * P],
                                   start=blk == 0, stop=blk == NT - 1)
                mm.then_inc(probs_summed, 1)

            def turn_sums(q, qs):
                pe.wait_ge(sums_copied, q + 1)
                for t in range(2):
                    mm = pe.transpose(final[qs][:, t * P:(t + 1) * P], oT[:, t * P:(t + 1) * P], ident[:])
                mm.then_inc(fin_turned, 1)

            def pair(q, qs, first, last=False):
                for v in range(VU):
                    turn1(q, qs, v, first)
                    if v == 0 and not first:
                        gather1(q - 1, 1 - qs, VU - 1)
                    if v >= 1:
                        gather1(q, qs, v - 1)
                    n = 4 * q + 5 + v // 3
                    if not last or n < 2 * NT:
                        if v % 3 == 0:
                            open_leaky(n)
                        if v % 3 == 1:
                            add_r(n, (v // 3 + 1) % 2)
                    if v == 2 and not first:
                        turn_sums(q - 1, 1 - qs)

            pe.wait_ge(epi_vec.sem, epi_vec.all(NG))
            pe.wait_ge(epi_act.sem, epi_act.all(NG))
            pair(0, 0, True)
            pair(1, 1, False)
            with pe.Fori(1, NI - 1) as i:
                pair(2 * i, 0, False)
                pair(2 * i + 1, 1, False)
            pair(NQ - 2, 0, False, last=True)
            pair(NQ - 1, 1, False, last=True)
            gather1(NQ - 1, 1, VU - 1)
            turn_sums(NQ - 1, 1)

        @block.vector
        def _(vec):
            def ln_center(steps, n, tag, src, center, stat, tl):
                ssum, nmean = stat[:2]

                def done(name):
                    vec.wait_ge(steps.sem, steps.at(n, name))

                vec.tensor_reduce(ssum, src, AX.X, ALU.add).then_inc(steps.sem, 1)
                done(f"sum_{tag}")
                vec.tensor_scalar(nmean, ssum, -1.0 / D, None, ALU.mult).then_inc(steps.sem, 1)
                done(f"mean_{tag}")
                vec.tensor_tensor(tiles(center, tl), src, per_tile(nmean, D), ALU.add).then_inc(steps.sem, 1)

            def ln_power(steps, acts, n, tag, sq_, stat, tl):
                _, _, power, _, _, var, _, _, _, _ = stat
                vec.wait_ge(acts.sem, acts.at(n, f"square_{tag}"))
                vec.tensor_reduce(power, tiles(sq_, tl), AX.X, ALU.add).then_inc(steps.sem, 1)
                vec.wait_ge(steps.sem, steps.at(n, f"power_{tag}"))
                vec.tensor_scalar(var, power, 1.0 / D, LN_EPS, ALU.mult, ALU.add).then_inc(steps.sem, 1)

            def ln_rstd(steps, acts, n, tag, stat, var_steps):
                _, _, _, _, seed, var, s2, s2v, fix, rstd = stat

                def done(name):
                    vec.wait_ge(steps.sem, steps.at(n, name))

                vec.wait_ge(var_steps.sem, var_steps.at(n, f"var_{tag}"))
                vec.wait_ge(acts.sem, acts.at(n, f"seed_{tag}"))
                vec.tensor_tensor(s2, seed, seed, ALU.mult).then_inc(steps.sem, 1)
                done(f"seed2_{tag}")
                vec.tensor_tensor(s2v, s2, var, ALU.mult).then_inc(steps.sem, 1)
                done(f"seed2var_{tag}")
                vec.tensor_scalar(fix, s2v, -0.5, 1.5, ALU.mult, ALU.add).then_inc(steps.sem, 1)
                done(f"fix_{tag}")
                vec.tensor_tensor(rstd, seed, fix, ALU.mult).then_inc(steps.sem, 1)
                done(f"rstd_{tag}")

            vec.memset(eps[:, 0:1], LN_EPS).then_inc(noise_vec.sem, 1)
            vec.memset(eps[:, 1:2], U_FLOOR).then_inc(noise_vec.sem, 1)
            vec.memset(ones[:], 1.0).then_inc(noise_vec.sem, 1)

            def widen():
                vec.wait_ge(consts_in, 16 * CONSTS)
                vec.tensor_scalar(a_wide[:, P:P + 1], vecs[:, 0:1], UNIT, None, ALU.mult).then_inc(attend.sem, 1)
                vec.tensor_scalar(a_wide[:, 0:P], vecs[:, 1:2].broadcast_to([P, P]), UNIT, None,
                                  ALU.mult).then_inc(attend.sem, 1)
                vec.tensor_copy(b_wide[:], vecs[:, 2:3].broadcast_to([P, P])).then_inc(attend.sem, 1)
                vec.wait_ge(ident_ready, 9)
                vec.tensor_copy(pick_r[:], pick).then_inc(bias_ready, 1)
                vec.tensor_copy(one_row_r[:], one_row).then_inc(bias_ready, 1)
                vec.tensor_copy(tiles(bcat_hi, 2), per_column(bcat, 2)).then_inc(bias_ready, 1)
                vec.wait_ge(bias_ready, 3)
                vec.tensor_tensor(tiles(bcat_lo, 2), per_column(bcat, 2), tiles(bcat_hi, 2).bitcast(F32),
                                  ALU.subtract).then_inc(bias_ready, 1)
                vec.wait_ge(noise_in, 32)
                vec.tensor_scalar(noise[:], noise[:], U_FLOOR, 1.0, ALU.max, ALU.min).then_inc(noise_vec.sem, 1)

            def keep_products():
                vec.wait_ge(wT_turned, 1)
                vec.tensor_copy(wT[:], ep[2][:, P:2 * P]).then_inc(attend.sem, 1)
                vec.tensor_copy(wa[:], ep[1][:, 0:P + 1]).then_inc(attend.sem, 1)
                vec.tensor_copy(ba[:], ep[1][:, P + 1:P + 3]).then_inc(attend.sem, 1)
                vec.wait_ge(noise_act.sem, noise_act.at(0, "loglog"))
                vec.tensor_tensor(noise[:], per_column(bn_row[:], NT), noise[:], ALU.subtract).then_inc(noise_vec.sem, 1)

            def piece_center_x(n):
                vec.wait_ge(x_loaded[n % 2], 16 * (n // 2 + 1))
                ln_center(piece_vec["center_x"], n, "x", tiles(x8[n % 2], PTL), cx8, pstat[0], PTL)

            def piece_power_x(n):
                ln_power(piece_vec["power_x"], piece_act["square_x"], n, "x", sqx8, pstat[0], PTL)

            def piece_h(n):
                ps = piece_vec["h"]
                ln_rstd(ps, piece_act["seed_x"], n, "x", pstat[0], piece_vec["power_x"])
                if n >= 1:
                    vec.wait_ge(h_stored, 16 * n)
                vec.scalar_tensor_tensor(tiles(h8, PTL), tiles(cx8, PTL), 0.0, per_tile(pstat[0][9], D),
                                         ALU.max, ALU.mult).then_inc(ps.sem, 1)

            def piece_center_h(n):
                vec.wait_ge(*piece_vec.at(n, "h"))
                if n >= 1:
                    vec.wait_ge(*piece_act.at(n - 1, f"normed{PTL - 1}"))
                ln_center(piece_vec["center_h"], n, "h", tiles(h8, PTL), ch8, pstat[1], PTL)

            def piece_power_h(n):
                ln_power(piece_vec["power_h"], piece_act["square_h"], n, "h", sqh8, pstat[1], PTL)

            def piece_rstd_h(n):
                ln_rstd(piece_vec["rstd_h"], piece_act["seed_h"], n, "h", pstat[1], piece_vec["power_h"])

            def piece_xn(n):
                ps, xn = piece_vec["xn"], tiles(xn8[n % 2], PTL)
                vec.wait_ge(*piece_act.at(n, f"normed{PTL - 1}"))
                vec.tensor_tensor(xn, xn, per_column(ROW["g_in"], PTL), ALU.mult).then_inc(ps.sem, 1)
                vec.wait_ge(*piece_vec.at(n, "scaled"))
                vec.tensor_tensor(xn, xn, per_column(ROW["b_in"], PTL), ALU.add).then_inc(ps.sem, 1)

            z, e = zbuf[:, 0], zbuf[:, 1]
            zmax, esum, erec, p1, hard, ysum = (zstat[:, i, :] for i in range(6))

            def piece_z(n):
                ps = piece_vec["z"]
                if n == 0:
                    vec.wait_ge(noise_vec.sem, noise_vec.at(0, "bias"))
                else:
                    vec.wait_ge(*piece_vec.at(n - 1, "hard"))
                vec.wait_ge(*piece_pe.at(n, "logits"))
                vec.tensor_tensor(z, ep[2][:, 0:2 * PTL].rearrange("p (t k) -> p t k", k=2),
                                  noise[:, n * PTL:(n + 1) * PTL, :], ALU.add).then_inc(ps.sem, 1)
                vec.wait_ge(*piece_vec.at(n, "z"))
                vec.tensor_tensor(zmax, z[:, :, 0], z[:, :, 1], ALU.max).then_inc(ps.sem, 1)
                vec.wait_ge(*piece_vec.at(n, "zmax"))
                vec.tensor_tensor(z, z, per_tile(zmax, 2), ALU.subtract).then_inc(ps.sem, 1)

            def piece_gate(n):
                ps = piece_vec["gate"]

                def done(name):
                    vec.wait_ge(*piece_vec.at(n, name))

                vec.wait_ge(*piece_act.at(n, "exp"))
                vec.tensor_tensor(esum, e[:, :, 0], e[:, :, 1], ALU.add).then_inc(ps.sem, 1)
                done("esum")
                vec.reciprocal(erec, esum).then_inc(ps.sem, 1)
                done("erec")
                vec.tensor_tensor(p1, e[:, :, 1], erec, ALU.mult).then_inc(ps.sem, 1)
                vec.tensor_tensor(hard, z[:, :, 1], z[:, :, 0], ALU.is_gt).then_inc(ps.sem, 1)
                done("hard")
                vec.tensor_tensor(ysum, hard, p1, ALU.add).then_inc(ps.sem, 1)
                done("y")
                vec.tensor_tensor(gate[:, n * PTL:(n + 1) * PTL], ysum, p1, ALU.subtract).then_inc(ps.sem, 1)

            def piece_gated(n):
                vec.wait_ge(*piece_vec.at(n, "gate"))
                xn = tiles(xn8[n % 2], PTL)
                vec.wait_ge(*piece_pe.at(n, "turn1"))
                vec.tensor_tensor(xn, xn, per_tile(gate[:, n * PTL:(n + 1) * PTL], D), ALU.mult).then_inc(piece_vec["gated"].sem, 1)

            def piece_lo(n):
                here = slice(n * PTL, (n + 1) * PTL)
                vec.wait_ge(*piece_act.at(n, "hi"))
                vec.tensor_tensor(gated_lo[:, here, :], tiles(xn8[n % 2], PTL), gated_hi[:, here, :].bitcast(F32),
                                  ALU.subtract).then_inc(piece_vec["lo"].sem, 1)

            piece_parts = {0: piece_center_x, 1: piece_power_x, 2: piece_h, 3: piece_center_h, 4: piece_power_h,
                           5: piece_rstd_h, 6: piece_xn, 9: piece_z, 10: piece_gate, 11: piece_gated,
                           12: piece_lo}

            def evacuate(g, v):
                vec.wait_ge(hi_ready[v % 2], g * (UG // 2) + v // 2 + 1)
                vec.tensor_tensor(turned_lo[v % 2][:], turning0[v % 2], turned_hi[v % 2][:].bitcast(F32),
                                  ALU.subtract).then_inc(lo_ready[v % 2], 1)

            v1 = carry_in[:, :, P:2 * P]
            hres = carry_in[:, :, 2 * P:3 * P]

            def epi_parts(g):
                es = epi_vec

                def done(name):
                    vec.wait_ge(es.sem, es.at(g, name))

                def gate_pre():
                    vec.wait_ge(carry_loaded, 32 * (g + 1))
                    for t in range(GT):
                        if t % 2 == 0:
                            vec.wait_ge(epi_pe.sem, epi_pe.at(g, ("mix01", "mix23")[t // 2]))
                        ps = ep[t // 2][:, (t % 2) * 2 * P:(t % 2) * 2 * P + P]
                        vec.scalar_tensor_tensor(tiles(fg)[:, t, :], ps, gate[:, bass.ds(g * GT + t, 1)],
                                                 carry_in[:, t, 0:P], ALU.mult, ALU.add).then_inc(es.sem, 1)

                def view2():
                    for t in range(GT):
                        ps = ep[t // 2][:, (t % 2) * 2 * P + P:(t % 2 + 1) * 2 * P]
                        vec.scalar_tensor_tensor(tiles(v2)[:, t, :], ps, gate[:, bass.ds(g * GT + t, 1)],
                                                 ROW["b2"], ALU.mult, ALU.add).then_inc(es.sem, 1)

                def gap():
                    done(f"view2_{GT - 1}")
                    vec.tensor_tensor(tiles(dlt), v1, tiles(v2), ALU.subtract).then_inc(es.sem, 1)
                    vec.wait_ge(epi_act.sem, epi_act.at(g, "exp"))
                    vec.tensor_scalar(fg, fg, 1.0, None, ALU.add).then_inc(es.sem, 1)

                def sigmoid(t):
                    done("one_plus")
                    part = fg[:, t * P:(t + 1) * P]
                    vec.reciprocal(part, part).then_inc(es.sem, 1)

                def fuse():
                    done(f"sigmoid{GT - 1}")
                    vec.tensor_tensor(dlt, dlt, fg, ALU.mult).then_inc(es.sem, 1)
                    done("mixed")
                    vec.tensor_tensor(y, v2, dlt, ALU.add).then_inc(es.sem, 1)

                def resid():
                    done("fused")
                    vec.tensor_tensor(tiles(y), tiles(y), hres, ALU.add).then_inc(es.sem, 1)

                def center_out():
                    done("resid")
                    ln_center(es, g, "out", tiles(y), dlt, estat, GT)

                def norm_out():
                    ln_rstd(es, epi_act, g, "out", estat, es)
                    vec.tensor_tensor(tiles(y), tiles(dlt), per_tile(estat[9], D), ALU.mult).then_inc(es.sem, 1)

                def scale_out():
                    done("normed")
                    vec.tensor_tensor(tiles(y), tiles(y), per_column(ROW["g_out"], GT), ALU.mult).then_inc(es.sem, 1)
                    done("scaled")
                    vec.tensor_tensor(tiles(y), tiles(y), per_column(ROW["b_out"], GT), ALU.add).then_inc(es.sem, 1)

                def to_x_mid():
                    done("shifted")
                    vec.tensor_tensor(y, y, x_in, ALU.add).then_inc(es.sem, 1)

                def center_next():
                    done("x_mid")
                    ln_center(es, g, "next", tiles(y), dlt, estat, GT)

                def norm_next():
                    ln_rstd(es, epi_act, g, "next", estat, es)
                    vec.scalar_tensor_tensor(tiles(h1), tiles(dlt), 0.0, per_tile(estat[9], D),
                                             ALU.max, ALU.mult).then_inc(es.sem, 1)

                def heads():
                    vec.wait_ge(epi_pe.sem, epi_pe.at(g, "H"))
                    vec.tensor_tensor(feats[:, bass.ts(g, GT), :], tiles(ep[0]), per_column(ROW["b"], GT),
                                      ALU.add).then_inc(es.sem, 1)
                    vec.wait_ge(epi_pe.sem, epi_pe.at(g, "s"))
                    met(vec)
                    vec.tensor_tensor(s_col[:, bass.ts(g, GT)], ep[2][:, 0:GT], ba[:, 1:2].broadcast_to([P, GT]),
                                      ALU.add).then_inc(es.sem, 1)
                    for part, name in ((1.0 - SLOPE, "s08"), (SLOPE, "s02")):
                        done("s")
                        vec.tensor_scalar({"s08": s08_col, "s02": s02_col}[name][:, bass.ts(g, GT)],
                                          s_col[:, bass.ts(g, GT)], part, None, ALU.mult).then_inc(es.sem, 1)

                return {2: [gate_pre], 3: [view2], 4: [gap],
                        5: [lambda: sigmoid(0)], 6: [lambda: sigmoid(1)], 7: [lambda: sigmoid(2)],
                        8: [lambda: sigmoid(3)], 9: [fuse], 10: [resid], 11: [center_out],
                        12: [lambda: ln_power(es, epi_act, g, "out", sq, estat, GT)],
                        13: [norm_out], 14: [scale_out], 15: [to_x_mid], 16: [center_next],
                        17: [lambda: ln_power(es, epi_act, g, "next", sq, estat, GT)],
                        18: [norm_next], 23: [heads]}

            for v in range(-LEAD, UG):
                if v >= 0:
                    evacuate(0, v)
                for part, n in due(piece_parts, v):
                    part(n)
                if v == 2 - LEAD:
                    widen()
                if v == 4 - LEAD:
                    keep_products()
            with vec.Fori(1, NG) as g:
                todo = epi_parts(g - 1)
                for v in range(UG):
                    evacuate(g, v)
                    for part in todo.get(v, ()):
                        part()

            def score_product(i, s, c):
                n = nth(i, s, c)
                cols = slice(c * HALF + LW, (c + 1) * HALF)
                vec.wait_ge(half_full[s][c], 16 * len(LOADS[c]) * (i + 1))
                vec.wait_ge(mask_ready, n + 1)
                vec.scalar_tensor_tensor(slot[s][:, cols], r_row[:, cols], s_col[:, bass.ds(SLOTS1 * i + s, 1)],
                                         slot[s][:, cols], ALU.add, ALU.mult).then_inc(score_vec.sem, 1)

            def score_leaky(i, s, c):
                n = nth(i, s, c)
                first, rest = (slot[s][:, c * HALF:c * HALF + LW], slot[s][:, c * HALF + LW:(c + 1) * HALF])
                vec.wait_ge(w_ready, n + 1)
                vec.scalar_tensor_tensor(first, leaky, s02_col[:, bass.ds(SLOTS1 * i + s, 1)], first,
                                         ALU.add, ALU.mult).then_inc(score_vec.sem, 1)
                vec.wait_ge(score_vec.sem, score_vec.at(n, "product"))
                vec.scalar_tensor_tensor(rest, rest, SLOPE, rest, ALU.mult, ALU.max).then_inc(score_vec.sem, 1)

            def score_max(i, s, c):
                n = nth(i, s, c)
                half = slot[s][:, c * HALF:(c + 1) * HALF]
                buf = n % 2 if isinstance(n, int) else c
                vec.wait_ge(score_vec.sem, score_vec.at(n, "leaky"))
                met(vec)
                vec.tensor_tensor_reduce(half, half, mask[buf][:], 1.0, LOWEST, ALU.subtract, ALU.max,
                                         maxes[:, s, c:c + 1]).then_inc(half_max, 1)

            def score(i, s, c):
                score_product(i, s, c)
                score_leaky(i, s, c)
                score_max(i, s, c)

            def row_max(i, s):
                vec.wait_ge(half_max, nth(i, s, 1) + 1)
                vec.tensor_reduce(top[:], maxes[:, s, :], AX.X, ALU.max).then_inc(top_ready, 1)
                vec.wait_ge(top_ready, SLOTS1 * i + s + 1)
                vec.tensor_scalar(negmax[:, s:s + 1], top[:], -1.0 / UNIT, None, ALU.mult).then_inc(max_ready, 1)

            def finish(q, qs):
                fv = fin_vec
                vec.wait_ge(exp_done, 4 * (q + 1))
                vec.tensor_reduce(rinv[:], sums[:, 2 * qs:2 * qs + 2, :], AX.X, ALU.add).then_inc(fv.sem, 1)
                vec.wait_ge(fv.sem, fv.at(q, "total"))
                vec.reciprocal(rinv[:], rinv[:]).then_inc(fv.sem, 1)
                vec.wait_ge(fv.sem, fv.at(q, "rinv"))
                vec.wait_ge(fin_turned, q + 1)
                vec.wait_ge(xm_loaded, 16 * (q + 1))
                if not (isinstance(q, int) and q == 0):
                    vec.wait_ge(out_stored, 16 * q)
                vec.tensor_tensor(fin[:], tiles(final[qs], 2), per_tile(rinv[:], P), ALU.mult).then_inc(fv.sem, 1)
                vec.wait_ge(fv.sem, fv.at(q, "scaled"))
                vec.tensor_tensor(fin[:], fin[:], x1_in[:], ALU.add).then_inc(fv.sem, 1)

            def step(i, s, first):
                q = 2 * i + s // 2 - 2
                score(i, s, 0)
                score(i, s, 1)
                if s % 2 == 0 and not first:
                    finish(q, s // 2)
                row_max(i, s)

            for c in range(2):
                here = slice(64 * c + 32, 64 * c + 64)
                vec.wait_ge(r_hi_ready, c + 1)
                vec.scalar_tensor_tensor(r_parts[here, :], r_row[here, c * HALF:c * HALF + LW], SLOPE,
                                         r_parts[here, :].bitcast(F32), ALU.mult, ALU.subtract).then_inc(r_lo_ready, 1)
            tail = epi_parts(NG - 1)
            meanwhile = {3: [lambda: score_product(0, 0, 0)], 11: [lambda: score_leaky(0, 0, 0)],
                         12: [lambda: score_max(0, 0, 0)], 16: [lambda: score_product(0, 1, 0)],
                         17: [lambda: score_leaky(0, 1, 0)], 18: [lambda: score_max(0, 1, 0)]}
            for v, parts in tail.items():
                for part in (*parts, *meanwhile.get(v, ())):
                    part()

            vec.wait_ge(epi_act.sem, epi_act.at(NG - 1, "r_row"))
            vec.wait_ge(epi_vec.sem, epi_vec.all(NG))
            for s in range(2):
                score(0, s, 1)
                row_max(0, s)
            for s in range(2, SLOTS1):
                step(0, s, True)
            with vec.Fori(1, NI) as i:
                for s in range(SLOTS1):
                    step(i, s, False)
            for q in (NQ - 2, NQ - 1):
                finish(q, q % 2)


_INS = ['x', 'adj', 'L0_gnn_u', 'L0_gnn_W1', 'L0_gnn_b1', 'L0_gnn_W2', 'L0_gnn_b2', 'L0_gnn_Wg', 'L0_gnn_bg',
        'L0_gnn_Wn', 'L0_gnn_bn', 'L0_gnn_g_in', 'L0_gnn_b_in', 'L0_gnn_g_out', 'L0_gnn_b_out',
        'L1_gnn_W', 'L1_gnn_b', 'L1_gnn_a_s', 'L1_gnn_a_r']


def kernel(**inputs):
    import numpy as _np
    import concourse.bacc as _bacc
    from concourse import mybir as _mybir
    from concourse.bass_utils import run_bass_kernel_spmd as _run

    nc = _bacc.Bacc("TRN2", target_bir_lowering=False, num_devices=1)
    arrays, args = {}, []
    for name in _INS:
        a = _np.ascontiguousarray(inputs[name])
        arrays[f"in_{name}_dram"] = a
        args.append(nc.dram_tensor(f"in_{name}_dram", a.shape, _mybir.dt.from_np(a.dtype), kind="ExternalInput").ap())
    out = nc.dram_tensor("out_dram", inputs["x"].shape, _mybir.dt.float32, kind="ExternalOutput").ap()
    build(nc, *args, out)
    r = _run(nc, [arrays], core_ids=[0])
    return r.results[0]["out_dram"]
```
